# Optimizing a Trainium2 kernel written in Bass

```python
import numpy as np
import jax
import jax.numpy as jnp

def _softmax(x, axis=-1):
    return jax.nn.softmax(x, axis=axis)

def _gelu(x):
    return jax.nn.gelu(x, approximate=True)

def _silu(x):
    return jax.nn.silu(x)

def _sigmoid(x):
    return jax.nn.sigmoid(x)

def _layernorm(x, axis=-1, eps=1e-05):
    m = jnp.mean(x, axis=axis, keepdims=True)
    v = jnp.var(x, axis=axis, keepdims=True)
    return (x - m) / jnp.sqrt(v + eps)

def _scatter_add(tgt, idx, src, axis=0):
    return tgt.at[idx].add(src)

def _segment_sum(src, seg, n):
    return jax.ops.segment_sum(src, seg, n)
kernel_name = 'mk_perceiver_d1_seqx_r4_cfa680'

def setup_inputs(seed: int=0):
    np.random.seed(seed)
    _w = jnp.asarray

    def _rec_inputs():
        import jax
        import jax.numpy as jnp
        _rk = jax.random.key(seed)
        x = -0.0003929 + 0.9999 * jax.random.normal(jax.random.fold_in(_rk, 1), (128, 32, 256), jnp.float32)
        _lenS = 32 - jax.random.randint(jax.random.fold_in(_rk, 7), (128,), 0, max(1, 32 // 4) + 1, jnp.int32)
        _lenS2 = 257 - jax.random.randint(jax.random.fold_in(_rk, 8), (128,), 0, max(1, 257 // 4) + 1, jnp.int32)
        _ctx_512P = jax.random.normal(jax.random.fold_in(_rk, 11), (128, 16, 128), jnp.float32)
        _ctx_512c = jax.random.dirichlet(jax.random.fold_in(_rk, 511), 0.3 * jnp.ones((16,), jnp.float32), (128, 257))
        _ctx_512t = jnp.einsum('bsk,bkd->bsd', _ctx_512c, _ctx_512P)
        _ctx_512t = _ctx_512t * jax.lax.rsqrt(jnp.mean(jnp.square(_ctx_512t)) + 1e-12) * 0.953939
        ctx_512 = -1.39393e-06 + 0.999914 * (_ctx_512t + 0.3 * jax.random.normal(jax.random.fold_in(_rk, 611), (128, 257, 128), jnp.float32))
        return (x, ctx_512)
    x, ctx_512 = _rec_inputs()

    def _L0_xattn_setup():
        import jax, jax.numpy as jnp
        import numpy as np
        HEADS = 16
        D_MODEL = 256
        IMG_MODEL = 128
        D_K = D_MODEL // HEADS
        key = jax.random.key(seed)
        ks = jax.random.split(key, 12)
        B, LQ, LKV = (8, 512, 256)
        s_dm = 1.0 / np.sqrt(D_MODEL)
        s_im = 1.0 / np.sqrt(IMG_MODEL)
        return {'q': jax.random.normal(ks[0], (B, LQ, D_MODEL), jnp.float32), 'k': jax.random.normal(ks[1], (B, LKV, IMG_MODEL), jnp.float32), 'v': jax.random.normal(ks[2], (B, LKV, IMG_MODEL), jnp.float32), 'Wq': jax.random.normal(ks[3], (D_MODEL, D_MODEL), jnp.float32) * s_dm, 'bq': jnp.zeros((D_MODEL,), jnp.float32), 'Wk': jax.random.normal(ks[4], (IMG_MODEL, D_MODEL), jnp.float32) * s_im, 'bk': jnp.zeros((D_MODEL,), jnp.float32), 'Wv': jax.random.normal(ks[5], (IMG_MODEL, D_MODEL), jnp.float32) * s_im, 'bv': jnp.zeros((D_MODEL,), jnp.float32), 'Wo': jax.random.normal(ks[6], (D_MODEL, D_MODEL), jnp.float32) * s_dm, 'bo': jnp.zeros((D_MODEL,), jnp.float32)}
    _L0_xattn_all = _L0_xattn_setup()
    _L0_xattn_in = {k: v for k, v in _L0_xattn_all.items() if k in ('Wq', 'bq', 'Wk', 'bk', 'Wv', 'bv', 'Wo', 'bo')}
    del _L0_xattn_all

    def _L0_attn_setup():
        import jax, jax.numpy as jnp
        import numpy as np
        D_MODEL = 256
        NUM_HEADS = 16
        LOCAL_WINDOW = 128
        GLOBAL_STRIDE = 64
        B, T = (4, 512)

        def _rope_tables(T, d_head, base=10000.0):
            half = d_head // 2
            pos = jnp.arange(T, dtype=jnp.float32)[:, None]
            inv_freq = 1.0 / base ** (jnp.arange(half, dtype=jnp.float32) / half)
            ang = pos * inv_freq[None, :]
            return (jnp.cos(ang), jnp.sin(ang))

        def _rope_apply(x, cos_h, sin_h):
            xe = x[..., 0::2]
            xo = x[..., 1::2]
            re = xe * cos_h - xo * sin_h
            ro = xe * sin_h + xo * cos_h
            return jnp.stack([re, ro], axis=-1).reshape(x.shape)
        key = jax.random.key(seed)
        k1, k2, k3 = jax.random.split(key, 3)
        x = jax.random.normal(k1, (B, T, D_MODEL), dtype=jnp.float32)
        W_qkv = jax.random.normal(k2, (D_MODEL, 3 * D_MODEL), dtype=jnp.float32) * D_MODEL ** (-0.5)
        W_out = jax.random.normal(k3, (D_MODEL, D_MODEL), dtype=jnp.float32) * D_MODEL ** (-0.5)
        b_out = jnp.zeros((D_MODEL,), dtype=jnp.float32)
        return {'x': x, 'W_qkv': W_qkv, 'W_out': W_out, 'b_out': b_out}
    _L0_attn_all = _L0_attn_setup()
    _L0_attn_in = {k: v for k, v in _L0_attn_all.items() if k in ('W_qkv', 'W_out', 'b_out')}
    del _L0_attn_all

    def _L0_ffn_setup():
        import jax, jax.numpy as jnp
        import numpy as np
        B, T, C = (4, 512, 256)
        E, F, K = (8, 512, 2)
        key = jax.random.key(seed)
        k0, k1, k2, k3 = jax.random.split(key, 4)
        s = lambda d: 1.0 / np.sqrt(d)
        x = jax.random.normal(k0, (B, T, C), dtype=jnp.float32)
        Wr = jax.random.normal(k1, (E, C), dtype=jnp.float32) * s(C)
        W1 = jax.random.normal(k2, (E, 2 * F, C), dtype=jnp.float32) * s(C)
        W2 = jax.random.normal(k3, (E, C, F), dtype=jnp.float32) * s(F)
        return {'x': x, 'Wr': Wr, 'W1': W1, 'W2': W2}
    _L0_ffn_all = _L0_ffn_setup()
    _L0_ffn_in = {k: v for k, v in _L0_ffn_all.items() if k in ('Wr', 'W1', 'W2')}
    del _L0_ffn_all
    return {'x': x, 'ctx_512': ctx_512, 'L0_xattn_Wq': _L0_xattn_in['Wq'], 'L0_xattn_bq': _L0_xattn_in['bq'], 'L0_xattn_Wk': _L0_xattn_in['Wk'], 'L0_xattn_bk': _L0_xattn_in['bk'], 'L0_xattn_Wv': _L0_xattn_in['Wv'], 'L0_xattn_bv': _L0_xattn_in['bv'], 'L0_xattn_Wo': _L0_xattn_in['Wo'], 'L0_xattn_bo': _L0_xattn_in['bo'], 'L0_attn_W_qkv': _L0_attn_in['W_qkv'], 'L0_attn_W_out': _L0_attn_in['W_out'], 'L0_attn_b_out': _L0_attn_in['b_out'], 'L0_ffn_Wr': _L0_ffn_in['Wr'], 'L0_ffn_W1': _L0_ffn_in['W1'], 'L0_ffn_W2': _L0_ffn_in['W2']}

def reference(x, ctx_512, L0_xattn_Wq, L0_xattn_bq, L0_xattn_Wk, L0_xattn_bk, L0_xattn_Wv, L0_xattn_bv, L0_xattn_Wo, L0_xattn_bo, L0_attn_W_qkv, L0_attn_W_out, L0_attn_b_out, L0_ffn_Wr, L0_ffn_W1, L0_ffn_W2):
    import jax
    import jax.numpy as jnp

    def _L0_xattn_ref(q, k, v, Wq, bq, Wk, bk, Wv, bv, Wo, bo):
        import jax, jax.numpy as jnp
        import numpy as np
        HEADS = 16
        D_MODEL = 256
        IMG_MODEL = 128
        D_K = D_MODEL // HEADS
        B, LQ, _ = q.shape
        LKV = k.shape[1]
        qh = (q @ Wq + bq).reshape(B, LQ, HEADS, D_K).transpose(0, 2, 1, 3)
        kh = (k @ Wk + bk).reshape(B, LKV, HEADS, D_K).transpose(0, 2, 1, 3)
        vh = (v @ Wv + bv).reshape(B, LKV, HEADS, D_K).transpose(0, 2, 1, 3)
        scale = 1.0 / np.sqrt(D_K)
        scores = jnp.einsum('bhqd,bhkd->bhqk', qh, kh) * scale
        attn = jax.nn.softmax(scores, axis=-1)
        out = jnp.einsum('bhqk,bhkd->bhqd', attn, vh)
        concat = out.transpose(0, 2, 1, 3).reshape(B, LQ, D_MODEL)
        return concat @ Wo + bo

    def _L0_attn_ref(x, W_qkv, W_out, b_out):
        import jax, jax.numpy as jnp
        import numpy as np
        D_MODEL = 256
        NUM_HEADS = 16
        LOCAL_WINDOW = 128
        GLOBAL_STRIDE = 64
        B, T = (4, 512)

        def _rope_tables(T, d_head, base=10000.0):
            half = d_head // 2
            pos = jnp.arange(T, dtype=jnp.float32)[:, None]
            inv_freq = 1.0 / base ** (jnp.arange(half, dtype=jnp.float32) / half)
            ang = pos * inv_freq[None, :]
            return (jnp.cos(ang), jnp.sin(ang))

        def _rope_apply(x, cos_h, sin_h):
            xe = x[..., 0::2]
            xo = x[..., 1::2]
            re = xe * cos_h - xo * sin_h
            ro = xe * sin_h + xo * cos_h
            return jnp.stack([re, ro], axis=-1).reshape(x.shape)
        Bx, Tx, C = x.shape
        H = NUM_HEADS
        dh = C // H
        qkv = x @ W_qkv
        qkv = qkv.reshape(Bx, Tx, 3, H, dh)
        q, k, v = (qkv[:, :, 0], qkv[:, :, 1], qkv[:, :, 2])
        q = jnp.transpose(q, (0, 2, 1, 3))
        k = jnp.transpose(k, (0, 2, 1, 3))
        v = jnp.transpose(v, (0, 2, 1, 3))
        cos_h, sin_h = _rope_tables(Tx, dh)
        q = _rope_apply(q, cos_h, sin_h)
        k = _rope_apply(k, cos_h, sin_h)
        scores = jnp.einsum('bhtd,bhkd->bhtk', q, k) / jnp.sqrt(jnp.float32(dh))
        lw = min(LOCAL_WINDOW, Tx)
        gs = max(1, GLOBAL_STRIDE)
        q_idx = jnp.arange(Tx)
        k_idx = jnp.arange(Tx)
        rel = k_idx[None, :] - q_idx[:, None]
        local_ok = (rel <= 0) & (rel >= -(lw - 1))
        key_global = (k_idx % gs == 0)[None, :]
        query_is_global = (q_idx % gs == 0)[:, None]
        allowed = (local_ok | key_global | query_is_global) & (rel <= 0)
        allowed = allowed[None, None, :, :]
        scores = jnp.where(allowed, scores, jnp.float32(-1000000000.0))
        w = jax.nn.softmax(scores, axis=-1)
        out = jnp.einsum('bhtk,bhkd->bhtd', w, v)
        out = jnp.transpose(out, (0, 2, 1, 3)).reshape(Bx, Tx, C)
        return out @ W_out + b_out

    def _L0_ffn_ref(x, Wr, W1, W2):
        import jax, jax.numpy as jnp
        import numpy as np
        B, T, C = (4, 512, 256)
        E, F, K = (8, 512, 2)
        Bb, Tt, Cc = x.shape
        flat = x.reshape(-1, Cc)
        N = flat.shape[0]
        logits = flat @ Wr.T
        weights, ids = jax.lax.top_k(logits, K)
        weights = jax.nn.softmax(weights, axis=-1)
        rows = jnp.arange(N)[:, None]
        router_weights = jnp.zeros((N, E), dtype=flat.dtype).at[rows, ids].add(weights)
        h = jnp.einsum('nc,efc->nef', flat, W1)
        val, gate = (h[..., :F], h[..., F:])
        act = val * jax.nn.silu(gate)
        expert_outputs = jnp.einsum('nef,ecf->nec', act, W2)
        out = jnp.einsum('nec,ne->nc', expert_outputs, router_weights)
        return out.reshape(Bb, Tt, Cc)
    x = x + _L0_xattn_ref(_layernorm(x, axis=-1), ctx_512, ctx_512, L0_xattn_Wq, L0_xattn_bq, L0_xattn_Wk, L0_xattn_bk, L0_xattn_Wv, L0_xattn_bv, L0_xattn_Wo, L0_xattn_bo)
    x = x + _L0_attn_ref(_layernorm(x, axis=-1), L0_attn_W_qkv, L0_attn_W_out, L0_attn_b_out)
    x = x + _L0_ffn_ref(_layernorm(x, axis=-1), L0_ffn_Wr, L0_ffn_W1, L0_ffn_W2)
    return x

_drawn_inputs = setup_inputs


def setup_inputs(seed=0):
    import zlib

    import numpy as np

    out = dict(_drawn_inputs(seed))
    spreads = {'L0_xattn_bq': (0.0, 0.1),
     'L0_xattn_bk': (0.0, 0.1),
     'L0_xattn_bv': (0.0, 0.1),
     'L0_xattn_bo': (0.0, 0.1),
     'L0_attn_b_out': (0.0, 0.1)}
    factors = {}
    for name, (base, spread) in spreads.items():
        noise = np.random.default_rng([zlib.crc32(name.encode()), seed]).standard_normal(out[name].shape)
        drawn = base * np.exp(spread * noise) if base else spread * noise
        out[name] = jnp.asarray(drawn.astype(out[name].dtype))
    for name, factor in factors.items():
        out[name] = (out[name] * factor).astype(out[name].dtype)
    return out
```

```python
from contextlib import ExitStack

import concourse.bass as bass
from concourse import mybir

F32 = mybir.dt.float32
F32R = mybir.dt.float32r
I32 = mybir.dt.int32
U32 = mybir.dt.uint32
ALU = mybir.AluOpType
ACT = mybir.ActivationFunctionType
AX_X = mybir.AxisListType.X

P = 128
Q = 32
D = 256
CD = 128
KV = 257
H = 16
DH = D // H
BT = P // Q
HC = H // 2
KT = 3
KROWS = (P, P, KV - 2 * P)
EPS = 1e-5
E = 8
F = 512
K = 2
DVE_LINKS = 30
POOL_LINKS = 4


def SLOT_TILES(tiles):
    return K * tiles + E


class Chain:

    def __init__(self, eng, sem):
        self.eng, self.sem, self.base, self.n = eng, sem, 0, 0

    def done(self, ins, wait=None):
        self.n += 1
        ins.then_inc(self.sem, 1)
        if wait:
            wait(self.eng, self.sem, self.base + self.n)
        else:
            self.eng.wait_ge(self.sem, self.base + self.n)


def perceiver(nc, x, ctxT, Wq, bq, Wk, bk, Wv, bvT, WoR, bo, Wqkv, Wout, bout, ident_d, hmask_d, cos_d, sin_d,
              causal_d, WrT, W1T, W2T, tri_d, rev_d, tid_d, out):
    TILES = x.shape[1]
    assert TILES % 4 == 0

    xs = nc.dram_tensor("slot_rows", (SLOT_TILES(TILES) * P, D), F32, kind="Internal").ap()
    ys = nc.dram_tensor("slot_outputs", (SLOT_TILES(TILES) * P, D), F32, kind="Internal").ap()

    with ExitStack() as whole:
        def kept(name, shape, dt=F32):
            return whole.enter_context(nc.sbuf_tensor(name, shape, dt))

        X = kept("X", [P, TILES, D])
        ident = kept("ident", [P, P])
        mhalf = kept("mhalf", [P, 1])
        attentions(nc, X, ident, mhalf, xs, x, ctxT, Wq, bq, Wk, bk, Wv, bvT, WoR, bo, Wqkv, Wout, bout, ident_d,
                   hmask_d, cos_d, sin_d, causal_d)
        experts(nc, X, ident, mhalf, xs, ys, WrT, W1T, W2T, tri_d, rev_d, tid_d, out)


def attentions(nc, X, ident, mhalf, xs, x, ctxT, Wq, bq, Wk, bk, Wv, bvT, WoR, bo, Wqkv, Wout, bout, ident_d,
               hmask_d, cos_d, sin_d, causal_d):
    TILES = X.shape[1]
    LAST = TILES - 1
    CW = BT * KV

    with ExitStack() as ctx:
        def sb(name, shape, dt=F32):
            return ctx.enter_context(nc.sbuf_tensor(name, shape, dt))

        def pb(name, shape, dt=F32):
            return ctx.enter_context(nc.psum_tensor(name, shape, dt))

        def sem(name):
            return ctx.enter_context(nc.semaphore(name))

        zeros = sb("zeros", [P, 8, D])
        cT = sb("cT", [P, 2, CW])
        wq = sb("wq", [P, 2, D])
        wk = sb("wk", [P, D])
        wv = sb("wv", [P, D])
        wo = sb("wo", [64, 4, D])
        wqkv = sb("wqkv", [P, 2, 3 * D])
        wout = sb("wout", [P, 2, D])
        bq_s = sb("bq_s", [P, 2])
        bk_s = sb("bk_s", [P, 2])
        bv_s = sb("bv_s", [64, 4])
        bo_s = sb("bo_s", [P, D])
        bout_s = sb("bout_s", [P, D])
        hmask = sb("hmask", [P, HC])
        cos_s = sb("cos_s", [P, DH])
        sin_s = sb("sin_s", [P, DH])
        causal = sb("causal", [P, Q])
        neg1 = sb("neg1", [P, P], F32R)
        stat = sb("stat", [P, 2, 6])
        mv = sb("mv", [P, 2, 2])
        rstd = sb("rstd", [P, 2])
        vareps = sb("vareps", [P, 2])
        xn1 = sb("xn1", [P, D])
        xT1 = sb("xT1", [P, 2, P])
        qT = sb("qT", [P, 2, 2, P])
        qblk = sb("qblk", [P, 2, 2, HC, Q])
        kT = sb("kT", [P, 2, 2, KV])
        vS = sb("vS", [P, 2, KT, H, DH + 1])
        mx = sb("mx", [P, 2, 4])
        mdiag = sb("mdiag", [P, 2, 4, P], F32R)
        pT = sb("pT", [P, 2, KT, H * Q])
        rs = sb("rs", [P, BT, 4])
        on = sb("on", [P, BT, 4, DH])
        oT = sb("oT", [64, 4, BT, Q])
        tmp = sb("tmp", [P, D])
        xn2 = sb("xn2", [P, D])
        xT2 = sb("xT2", [P, 2, P])
        rot = sb("rot", [P, 2 * D])
        swp = sb("swp", [P, 2 * D])
        v2 = sb("v2", [P, D])
        qkT = sb("qkT", [P, 4, P])
        qblk2 = sb("qblk2", [P, 2, BT, HC, Q])
        s2 = sb("s2", [P, H, Q])
        m2 = sb("m2", [P, H])
        r2 = sb("r2", [P, H])
        l2 = sb("l2", [P, H])
        pT2 = sb("pT2", [P, H * Q])
        o2 = sb("o2", [P, D])
        o2T = sb("o2T", [P, 2, P])

        psP = [pb(f"psP{i}", [P, 512]) for i in range(2)]
        psA = [pb(f"psA{i}", [P, 512]) for i in range(2)]
        psB = [pb(f"psB{i}", [P, 512]) for i in range(2)]
        psO = pb("psO", [P, 512])
        psX = pb("psX", [P, 512])
        oV = psO[:, 0:BT * 4 * (DH + 1)].rearrange("p (b g d) -> p b g d", b=BT, g=4)

        x_in = [sem("x_in0"), sem("x_in1")]
        w_in = sem("w_in")
        ctx_in = [sem("ctx_in0"), sem("ctx_in1")]
        ones_set = sem("ones_set")
        k_mm = sem("k_mm")
        k_ev = sem("k_ev")
        v_mm = sem("v_mm")
        v_ev = sem("v_ev")
        a_mm = sem("a_mm")
        max_done = sem("max_done")
        d_ready = sem("d_ready")
        sb_mm = sem("sb_mm")
        exp_done = sem("exp_done")
        pv_mm = sem("pv_mm")
        on_ready = sem("on_ready")
        q_ready = sem("q_ready")
        qblk_ready = sem("qblk_ready")
        var1 = sem("var1")
        var2 = sem("var2")
        rstd1 = sem("rstd1")
        rstd2 = sem("rstd2")
        ln1 = sem("ln1")
        step_mm = sem("step_mm")
        step_ready = sem("step_ready")
        tr_copied = sem("tr_copied")
        sub_done = sem("sub_done")
        exp2_done = sem("exp2_done")
        dve_chain = sem("dve_chain")
        pool_chain = sem("pool_chain")
        carried = sem("carried")
        x_out = sem("x_out")
        N_W = 16

        def wait_apart(eng, semaphore, value):
            eng.wait_ge(semaphore, value)
            if not isinstance(value, int):
                eng.sem_inc(carried, 1)

        def step_no(tau, k, first, last):
            if first:
                return 2 + k
            if last:
                return 4 + 12 * (LAST - 1) + k - 2
            return 4 + 12 * (tau - 1) + k

        def final_no(k):
            return 4 + 12 * (LAST - 1) + 10 + k

        def ctx_wait(eng, tau, par):
            eng.wait_ge(ctx_in[par], (tau - par) * 8 + 16)

        def over_tiles(eng, body):
            body(0, 0, True, False)
            with eng.Fori(0, (TILES - 2) // 2) as j:
                body(2 * j + 1, 1, False, False)
                body(2 * j + 2, 0, False, False)
            body(LAST, 1, False, True)

        block = ctx.enter_context(nc.Block())

        @block.sync
        def _(sp):
            sp.dma_start(X[:, 0:1, :], x[:, 0:1, :]).then_inc(x_in[0], 16)
            for dst, src in ((ident, ident_d), (wq, Wq), (bq_s, bq), (hmask, hmask_d), (wk, Wk), (wv, Wv),
                             (bk_s, bk)):
                sp.dma_start(dst[:], src).then_inc(w_in, 16)

            def load_ctx(tau, par):
                sp.dma_start(cT[:, par, :], ctxT[:, bass.ds(tau * CW, CW)]).then_inc(ctx_in[par], 16)

            load_ctx(0, 0)
            load_ctx(1, 1)
            sp.dma_start(X[:, 1:TILES, :], x[:, 1:TILES, :]).then_inc(x_in[1], 16)
            for dst, src in ((wo, WoR), (bv_s, bvT), (bo_s, bo), (wqkv, Wqkv), (cos_s, cos_d), (sin_s, sin_d),
                             (causal, causal_d), (wout, Wout), (bout_s, bout)):
                sp.dma_start(dst[:], src).then_inc(w_in, 16)
            with sp.Fori(0, (TILES - 2) // 2) as j:
                sp.wait_ge(v_mm, 16 * j + 8)
                load_ctx(2 * j + 2, 0)
                sp.wait_ge(v_mm, 16 * j + 16)
                load_ctx(2 * j + 3, 1)
            sp.wait_ge(ones_set, 3)
            for r in range(0, SLOT_TILES(TILES), 8):
                n = min(8, SLOT_TILES(TILES) - r)
                sp.dma_start(xs[r * P:(r + n) * P, :].rearrange("(p r) d -> p r d", p=P),
                             zeros[:, 0:n, :]).then_inc(x_out, 16)
            sp.wait_ge(x_out, 16 * (-(-SLOT_TILES(TILES) // 8)))

        @block.gpsimd
        def _(pool):
            chain = Chain(pool, pool_chain)
            chain.done(pool.memset(mhalf[:], -0.5))
            pool.wait_ge(w_in, 16 * N_W)

            def inv_std(k, tau, var, done):
                wait_apart(pool, var, tau + 1)
                chain.done(pool.tensor_scalar(vareps[:, k:k + 1], mv[:, k, 1:2], EPS, None, ALU.add))
                pool.tensor_tensor(rstd[:, k:k + 1], vareps[:, k:k + 1], mhalf[:], ALU.pow).then_inc(done, 1)

            def spread_q(tau, par, b):
                g = 4 * tau + b
                pool.wait_ge(q_ready, tau + 1)
                if not (isinstance(tau, int) and g < 2):
                    pool.wait_ge(sb_mm, 3 * (g - 1))
                src = qT[:, par, :, b * Q:(b + 1) * Q]
                pool.tensor_tensor(qblk[:, b % 2], src.unsqueeze(2).to_broadcast([P, 2, HC, Q]),
                                   hmask[:].unsqueeze(1).unsqueeze(3).to_broadcast([P, 2, HC, Q]),
                                   ALU.mult).then_inc(qblk_ready, 1)

            def spread_q2(n):
                pool.wait_ge(tr_copied, n)
                for c in range(2):
                    src = qkT[:, c, :].rearrange("p (b q) -> p b q", b=BT)
                    ins = pool.tensor_tensor(qblk2[:, c], src.unsqueeze(2).to_broadcast([P, BT, HC, Q]),
                                             hmask[:].unsqueeze(1).unsqueeze(3).to_broadcast([P, BT, HC, Q]),
                                             ALU.mult)
                ins.then_inc(step_ready, 1)

            def body(tau, par, first, last):
                for b in range(BT):
                    if b == 0 and not last:
                        inv_std(0, tau + 1, var1, rstd1)
                    if b == 3 and not last:
                        spread_q(tau + 1, 1 - par, 0)
                    elif b < 3:
                        spread_q(tau, par, b + 1)
                    if b == 1 and not first:
                        inv_std(1, tau - 1, var2, rstd2)
                    if b == 2 and not first:
                        spread_q2(tau)

            inv_std(0, 0, var1, rstd1)
            spread_q(0, 0, 0)
            body(0, 0, True, False)
            start = chain.n
            with pool.Fori(0, (TILES - 2) // 2) as j:
                chain.base = j * POOL_LINKS
                body(2 * j + 1, 1, False, False)
                body(2 * j + 2, 0, False, False)
            assert chain.n - start == POOL_LINKS, chain.n - start
            chain.base = ((TILES - 2) // 2 - 1) * POOL_LINKS
            body(LAST, 1, False, True)
            inv_std(1, LAST, var2, rstd2)
            spread_q2(LAST + 1)

        @block.scalar
        def _(act):
            act.wait_ge(w_in, 16 * N_W)

            def step_copy(dst, src, n, sem2=None):
                act.wait_ge(step_mm, n + 1)
                ins = act.activation(dst, src, ACT.Identity)
                ins.then_inc(sem2 or step_ready, 1)

            def x2v(t):
                return psX[:, 0:2 * P].rearrange("p (c n) -> p c n", c=2)

            def keys(g, par_g, first=False):
                for c in range(2):
                    act.wait_ge(k_mm, 2 * g + c + 1)
                    if not first:
                        act.wait_ge(sb_mm, 3 * (g - 1))
                    act.activation(kT[:, par_g, c, :], psP[c][:, 0:KV], ACT.Identity,
                                   bias=bk_s[:, c:c + 1]).then_inc(k_ev, 1)

            def exps(g, par_g, first=False):
                for t in range(KT):
                    r = KROWS[t]
                    act.wait_ge(sb_mm, 3 * g + t + 1)
                    if not first:
                        act.wait_ge(pv_mm, g - 1)
                    act.activation(pT[0:r, par_g, t, :], psB[(3 * par_g + t) % 2][0:r, :],
                                   ACT.Exp).then_inc(exp_done, 1)

            def slot(tau, k, first, last):
                n = step_no(tau, k, first, last)
                if k == 0 and not last:
                    step_copy(xT1[:], x2v(0), n)
                if first:
                    return
                epi(tau - 1, k - 2, n)

            def epi(tau, e, n):
                if e == 2:
                    step_copy(xT2[:], x2v(0), n)
                elif e == 4:
                    step_copy(v2[:], psX[:, 0:D], n)
                elif e == 5:
                    step_copy(qkT[:], psX[:, :].rearrange("p (c n) -> p c n", c=4), n, tr_copied)
                elif e == 6:
                    act.wait_ge(sub_done, tau + 1)
                    act.activation(s2[:], s2[:], ACT.Exp, scale=DH ** -0.5).then_inc(exp2_done, 1)
                elif e == 7:
                    step_copy(o2[:], psX[:, 0:D], n)
                elif e == 8:
                    step_copy(o2T[:], x2v(0), n)

            def body(tau, par, first, last):
                for b in range(BT):
                    g = 4 * tau + b
                    slot(tau, 3 * b, first, last)
                    if not (last and b == 3):
                        keys(g + 1, (b + 1) % 2, first=first and b == 0)
                    slot(tau, 3 * b + 1, first, last)
                    exps(g, b % 2, first=first and b < 2)
                    slot(tau, 3 * b + 2, first, last)

            step_copy(xT1[:], x2v(0), 0)
            keys(0, 0, first=True)
            over_tiles(act, body)
            for e in range(10):
                epi(LAST, e, final_no(e))

        @block.vector
        def _(dve):
            chain = Chain(dve, dve_chain)
            dve.memset(neg1[:].bitcast(F32), -1.0).then_inc(ones_set, 1)
            dve.memset(vS[:, :, :, :, DH:DH + 1], 1.0).then_inc(ones_set, 1)
            dve.memset(zeros[:], 0.0).then_inc(ones_set, 1)
            dve.wait_ge(x_in[0], 16)

            def norm(k, tau, src, dst, var, rdy, done):
                chain.done(dve.bn_stats(stat[:, k], src), wait_apart)
                dve.bn_aggr(mv[:, k], stat[:, k]).then_inc(var, 1)
                dve.wait_ge(var, tau + 1)
                dve.wait_ge(rdy, tau + 1)
                dve.tensor_scalar(dst, src, mv[:, k, 0:1], rstd[:, k:k + 1], ALU.subtract, ALU.mult).then_inc(done, 1)

            def xi(tau):
                return X[:, bass.ds(tau, 1), :].rearrange("p a d -> p (a d)")

            def query(tau, par, n, first):
                dve.wait_ge(step_mm, n + 1)
                if not first:
                    dve.wait_ge(qblk_ready, 4 * (tau - 1))
                chain.done(dve.tensor_tensor(qT[:, par], psX[:, 0:2 * P].rearrange("p (c n) -> p c n", c=2),
                                             bq_s[:].unsqueeze(2).to_broadcast([P, 2, P]), ALU.add))
                chain.done(dve.tensor_scalar(qT[:, par], qT[:, par], DH ** -0.5, None, ALU.mult))
                dve.sem_inc(q_ready, 1)
                dve.sem_inc(step_ready, 1)

            def values(g, par_g, first=False):
                dve.wait_ge(v_mm, 2 * g + 1)
                if not first:
                    dve.wait_ge(pv_mm, g - 1)
                dve.tensor_copy(vS[:, par_g, 0:2, :, 0:DH],
                                psP[0][:, :].rearrange("p (t h d) -> p t h d", t=2, h=H)).then_inc(v_ev, 1)
                dve.wait_ge(v_mm, 2 * g + 2)
                dve.tensor_copy(vS[0:1, par_g, 2, :, 0:DH],
                                psP[1][0:1, 0:D].rearrange("p (h d) -> p h d", h=H)).then_inc(v_ev, 1)

            def maxima(g, par_g, first=False):
                for a in range(4):
                    dve.wait_ge(a_mm, 4 * g + a + 1)
                    dve.reduce_max(mx[:, par_g, a:a + 1], psA[a % 2][:, 0:KV], AX_X).then_inc(max_done, 1)
                dve.wait_ge(max_done, 4 * g + 4)
                if not first:
                    dve.wait_ge(sb_mm, 3 * (g - 1))
                dve.tensor_tensor(mdiag[:, par_g], ident[:].unsqueeze(1).to_broadcast([P, 4, P]),
                                  mx[:, par_g].unsqueeze(2).to_broadcast([P, 4, P]),
                                  ALU.mult).then_inc(d_ready, 1)

            def norm_o(tau):
                dve.wait_ge(pv_mm, 4 * tau + 4)
                chain.done(dve.reciprocal(rs[:], oV[:, :, :, DH]))
                dve.tensor_tensor(on[:], oV[:, :, :, 0:DH], rs[:].unsqueeze(3).to_broadcast([P, BT, 4, DH]),
                                  ALU.mult).then_inc(on_ready, 1)

            def epi(tau, e, n):
                if e == 0:
                    dve.wait_ge(step_mm, n + 1)
                    dve.tensor_tensor(oT[:].rearrange("p c b q -> p b c q"),
                                      psX[0:64, :].rearrange("p (b c q) -> p b c q", b=BT, c=4),
                                      bv_s[:].unsqueeze(1).unsqueeze(3).to_broadcast([64, BT, 4, Q]),
                                      ALU.add).then_inc(step_ready, 1)
                elif e == 1:
                    dve.wait_ge(step_mm, n + 1)
                    chain.done(dve.tensor_tensor(tmp[:], psX[:, 0:D], bo_s[:], ALU.add))
                    chain.done(dve.tensor_tensor(xi(tau), xi(tau), tmp[:], ALU.add), wait_apart)
                    norm(1, tau, xi(tau), xn2[:], var2, rstd2, step_ready)
                elif e == 3:
                    dve.wait_ge(step_mm, n + 1)
                    ps = psX[:, :].rearrange("p (h f e) -> p h f e", f=DH // 2, e=2)
                    sv = swp[:].rearrange("p (h f e) -> p h f e", f=DH // 2, e=2)
                    sn = sin_s[:].rearrange("p (f e) -> p f e", e=2)
                    for e2 in range(2):
                        dve.tensor_tensor(sv[:, :, :, e2], ps[:, :, :, 1 - e2],
                                          sn[:, :, e2].unsqueeze(1).to_broadcast([P, 2 * H, DH // 2]), ALU.mult)
                    chain.done(dve.tensor_tensor(rot[:].rearrange("p (h d) -> p h d", d=DH),
                                                 psX[:, :].rearrange("p (h d) -> p h d", d=DH),
                                                 cos_s[:].unsqueeze(1).to_broadcast([P, 2 * H, DH]), ALU.mult))
                    dve.tensor_tensor(rot[:], rot[:], swp[:], ALU.add).then_inc(step_ready, 1)
                elif e == 6:
                    dve.wait_ge(step_mm, n + 1)
                    chain.done(dve.transpose(s2[:].rearrange("p h k -> p (h k)"), psX[:, :]))
                    chain.done(dve.tensor_tensor(s2[:], s2[:], causal[:].unsqueeze(1).to_broadcast([P, H, Q]), ALU.add))
                    chain.done(dve.reduce_max(m2[:], s2[:], AX_X))
                    dve.tensor_tensor(s2[:], s2[:], m2[:].unsqueeze(2).to_broadcast([P, H, Q]),
                                      ALU.subtract).then_inc(sub_done, 1)
                    dve.wait_ge(exp2_done, tau + 1)
                    chain.done(dve.reduce_sum(l2[:], s2[:], AX_X))
                    chain.done(dve.reciprocal(r2[:], l2[:]))
                    chain.done(dve.tensor_tensor(s2[:], s2[:], r2[:].unsqueeze(2).to_broadcast([P, H, Q]), ALU.mult))
                    dve.transpose(pT2[:], s2[:].rearrange("p h k -> p (h k)")).then_inc(step_ready, 1)
                elif e == 9:
                    dve.wait_ge(step_mm, n + 1)
                    chain.done(dve.tensor_tensor(tmp[:], psX[:, 0:D], bout_s[:], ALU.add))
                    dve.tensor_tensor(xi(tau), xi(tau), tmp[:], ALU.add).then_inc(step_ready, 1)

            def slot(tau, par, k, first, last):
                n = step_no(tau, k, first, last)
                if k == 1 and not last:
                    query(tau + 1, 1 - par, n, first)
                if not first:
                    epi(tau - 1, k - 2, n)

            def body(tau, par, first, last):
                for b in range(BT):
                    g = 4 * tau + b
                    if b == 0 and not last:
                        norm(0, tau + 1, xi(tau + 1), xn1[:], var1, rstd1, ln1)
                    maxima(g, b % 2, first=first and b < 2)
                    slot(tau, par, 3 * b, first, last)
                    if b == 0 and not first:
                        norm_o(tau - 1)
                    slot(tau, par, 3 * b + 1, first, last)
                    if not (last and b == 3):
                        values(g + 1, (b + 1) % 2, first=first and b == 0)
                    slot(tau, par, 3 * b + 2, first, last)

            dve.wait_ge(w_in, 16 * N_W)
            norm(0, 0, X[:, 0, :], xn1[:], var1, rstd1, ln1)
            dve.wait_ge(x_in[1], 16)
            query(0, 0, 1, True)
            values(0, 0, first=True)
            body(0, 0, True, False)
            start = chain.n
            with dve.Fori(0, (TILES - 2) // 2) as j:
                chain.base = j * DVE_LINKS
                body(2 * j + 1, 1, False, False)
                body(2 * j + 2, 0, False, False)
            assert chain.n - start == DVE_LINKS, chain.n - start
            chain.base = ((TILES - 2) // 2 - 1) * DVE_LINKS
            body(LAST, 1, False, True)
            norm_o(LAST)
            for e in range(10):
                epi(LAST, e, final_no(e))

        @block.tensor
        def _(pe):
            pe.wait_ge(ones_set, 2)
            pe.wait_ge(w_in, 16 * N_W)

            def keys(tau, par, b, first=False):
                g = 4 * tau + b
                if b == 0:
                    ctx_wait(pe, tau, par)
                for c in range(2):
                    if not first:
                        pe.wait_ge(v_ev, 2 * g - 1 + c)
                    pe.matmul(psP[c][:, 0:KV], wk[:, c * P:(c + 1) * P], cT[:, par, b * KV:(b + 1) * KV],
                              start=True, stop=True).then_inc(k_mm, 1)

            def values(tau, par, b):
                g = 4 * tau + b
                pe.wait_ge(k_ev, 2 * g + 1)
                for t in range(2):
                    mm = pe.matmul(psP[0][:, t * D:(t + 1) * D], cT[:, par, b * KV + t * P:b * KV + (t + 1) * P],
                                   wv[:], start=True, stop=True)
                mm.then_inc(v_mm, 1)
                pe.wait_ge(k_ev, 2 * g + 2)
                pe.matmul(psP[1][0:1, 0:D], cT[:, par, b * KV + 2 * P:(b + 1) * KV], wv[:],
                          start=True, stop=True).then_inc(v_mm, 1)

            def score_rows(g, par_g, first=False):
                pe.wait_ge(qblk_ready, g + 1)
                pe.wait_ge(k_ev, 2 * g + 2)
                for a in range(4):
                    if not (first and a < 2):
                        pe.wait_ge(max_done, 4 * g + a - 1)
                    pe.matmul(psA[a % 2][:, 0:KV], qblk[:, par_g, a // 2, 4 * (a % 2):4 * (a % 2) + 4, :],
                              kT[:, par_g, a // 2, :], start=True, stop=True).then_inc(a_mm, 1)

            def score_cols(g, par_g, first=False):
                pe.wait_ge(d_ready, g + 1)
                for t in range(KT):
                    r = KROWS[t]
                    bank = psB[(3 * par_g + t) % 2]
                    if not (first and t < 2):
                        pe.wait_ge(exp_done, 3 * g + t - 1)
                    pe.matmul(bank[:, :], neg1[:], mdiag[:, par_g], start=True, stop=False, skip_group_check=True)
                    for c in range(2):
                        mm = pe.matmul(bank[0:r, c * 256:(c + 1) * 256], kT[:, par_g, c, t * P:t * P + r],
                                       qblk[:, par_g, c], start=False, stop=True, skip_group_check=True)
                    mm.then_inc(sb_mm, 1)

            def weigh(g, par_g, b, tau, first_tile):
                pe.wait_ge(v_ev, 2 * g + 2)
                if b == 0 and not first_tile:
                    pe.wait_ge(on_ready, tau)
                pe.wait_ge(exp_done, 3 * g + 3)
                for t in range(KT):
                    r = KROWS[t]
                    for h in range(H):
                        c = h % 4
                        mm = pe.matmul(oV[32 * c:32 * c + 32, b, h // 4, :], pT[0:r, par_g, t, h * Q:(h + 1) * Q],
                                       vS[0:r, par_g, t, h, :], start=(b == 0 and t == 0 and h < 4), stop=(t == 2),
                                       skip_group_check=True)
                mm.then_inc(pv_mm, 1)

            def transposes(src, n, m=P):
                for i in range(n):
                    mm = pe.transpose(psX[0:m, i * P:(i + 1) * P], src(i), ident[:])
                mm.then_inc(step_mm, 1)

            def p_step(tau, k, n):
                if k == 0:
                    pe.wait_ge(ln1, tau + 1)
                    if n is not None:
                        pe.wait_ge(step_ready, n)
                    transposes(lambda i: xn1[:, i * P:(i + 1) * P], 2)
                else:
                    pe.wait_ge(step_ready, n)
                    for m in range(2):
                        for c in range(2):
                            mm = pe.matmul(psX[:, m * P:(m + 1) * P], wq[:, c, m * P:(m + 1) * P], xT1[:, c, :],
                                           start=(c == 0), stop=(c == 1))
                    mm.then_inc(step_mm, 1)

            def epi(tau, e, n):
                if not 0 <= e < 10:
                    return
                if e in (0, 7):
                    wait_apart(pe, step_ready, n)
                else:
                    pe.wait_ge(step_ready, n)
                if e == 0:
                    wait_apart(pe, on_ready, tau + 1)
                    transposes(lambda b: on[:, b].rearrange("p g d -> p (g d)"), BT, 64)
                elif e == 1:
                    for c in range(4):
                        mm = pe.matmul(psX[:, 0:D], oT[:, c], wo[:, c, :], start=(c == 0), stop=(c == 3))
                    mm.then_inc(step_mm, 1)
                elif e == 2:
                    transposes(lambda i: xn2[:, i * P:(i + 1) * P], 2)
                elif e in (3, 4):
                    w = 2 * D if e == 3 else D
                    o = 0 if e == 3 else 2 * D
                    for c in range(2):
                        mm = pe.matmul(psX[:, 0:w], xT2[:, c, :], wqkv[:, c, o:o + w], start=(c == 0), stop=(c == 1))
                    mm.then_inc(step_mm, 1)
                elif e == 5:
                    transposes(lambda i: rot[:, i * P:(i + 1) * P], 4)
                elif e == 6:
                    for b in range(BT):
                        for c in range(2):
                            mm = pe.matmul(psX[b * Q:(b + 1) * Q, c * 256:(c + 1) * 256],
                                           qkT[:, 2 + c, b * Q:(b + 1) * Q], qblk2[:, c, b], start=(c == 0), stop=True,
                                           skip_group_check=True)
                    mm.then_inc(step_mm, 1)
                elif e == 7:
                    for h in range(H):
                        for b in range(BT):
                            s = slice(b * Q, (b + 1) * Q)
                            mm = pe.matmul(psX[s, h * DH:(h + 1) * DH], pT2[s, h * Q:(h + 1) * Q],
                                           v2[s, h * DH:(h + 1) * DH], start=(h == 0), stop=True,
                                           skip_group_check=True)
                    mm.then_inc(step_mm, 1)
                elif e == 8:
                    transposes(lambda i: o2[:, i * P:(i + 1) * P], 2)
                elif e == 9:
                    for c in range(2):
                        mm = pe.matmul(psX[:, 0:D], o2T[:, c, :], wout[:, c, :], start=(c == 0), stop=(c == 1))
                    mm.then_inc(step_mm, 1)

            def slot(tau, k, first, last):
                n = step_no(tau, k, first, last)
                if k < 2 and not last:
                    p_step(tau + 1, k, n)
                if not first:
                    epi(tau - 1, k - 2, n)

            def body(tau, par, first, last):
                for b in range(BT):
                    g = 4 * tau + b
                    score_rows(g, b % 2, first=first and b == 0)
                    slot(tau, 3 * b, first, last)
                    if not (last and b == 3):
                        if b < 3:
                            keys(tau, par, b + 1)
                        else:
                            keys(tau + 1, 1 - par, 0)
                    if b > 0:
                        weigh(g - 1, (b - 1) % 2, b - 1, tau, first)
                    elif not first:
                        weigh(g - 1, 1, 3, tau - 1, False)
                    slot(tau, 3 * b + 1, first, last)
                    if b < 3:
                        values(tau, par, b + 1)
                    elif not last:
                        values(tau + 1, 1 - par, 0)
                    score_cols(g, b % 2, first=first and b == 0)
                    slot(tau, 3 * b + 2, first, last)

            p_step(0, 0, None)
            p_step(0, 1, 1)
            keys(0, 0, 0, first=True)
            values(0, 0, 0)
            over_tiles(pe, body)
            weigh(4 * LAST + 3, 1, 3, LAST, False)
            for e in range(10):
                epi(LAST, e, final_no(e))




def experts(nc, X, ident, mhalf, xs, ys, WrT, W1T, W2T, tri_d, rev_d, tid_d, out):
    TILES = X.shape[1]
    NS = SLOT_TILES(TILES)
    FC = F // P
    GS = min(8, TILES // 2)

    with ExitStack() as ctx:
        def sb(name, shape, dt=F32):
            return ctx.enter_context(nc.sbuf_tensor(name, shape, dt))

        def pb(name, shape, dt=F32):
            return ctx.enter_context(nc.psum_tensor(name, shape, dt))

        def sem(name):
            return ctx.enter_context(nc.semaphore(name))

        XN = sb("XN", [P, TILES, D])
        w1 = sb("w1", [P, E, 2, 2 * F])
        w2 = sb("w2", [P, E, FC, D])
        wr = sb("wr", [P, 2, E])
        tri = sb("tri", [P, P])
        ones = sb("ones", [P, P])
        rev = sb("rev", [P, E])
        tid = sb("tid", [1, NS])
        st3 = sb("st3", [P, TILES, 6])
        mean3 = sb("mean3", [P, TILES])
        sq3 = sb("sq3", [P, TILES])
        half3 = sb("half3", [P, TILES])
        var3 = sb("var3", [P, TILES])
        ve3 = sb("ve3", [P, TILES])
        rstd3 = sb("rstd3", [P, TILES])
        xb = sb("xb", [P, 2, D])
        xbT = sb("xbT", [P, 2, 2, P])
        lg = sb("lg", [P, TILES, E])
        lm = sb("lm", [P, TILES, E])
        eq = sb("eq", [P, TILES, E])
        top = sb("top", [P, K, TILES])
        first = sb("first", [P, K, TILES])
        hot = sb("hot", [P, K, TILES, E])
        both = sb("both", [P, TILES, E])
        gap = sb("gap", [P, TILES])
        egap = sb("egap", [P, TILES])
        wgt = sb("wgt", [P, K, TILES])
        tot = sb("tot", [P, TILES, E])
        scan = sb("scan", [P, 2, TILES, E])
        cnt_i = sb("cnt_i", [P, E], I32)
        cnt_t = sb("cnt_t", [P, E], I32)
        nt = sb("nt", [P, E])
        escan = sb("escan", [P, 2, E])
        base = sb("base", [P, E])
        posE = sb("posE", [P, TILES, E])
        posf = sb("posf", [P, K, TILES])
        pos = sb("pos", [P, K, TILES], U32)
        past = sb("past", [1, NS, E])
        tef = sb("tef", [1, NS])
        te = sb("te", [1, NS], I32)
        xrow = sb("xrow", [P, 2, D])
        xsT = sb("xsT", [P, 2, 2, P])
        sg = sb("sg", [P, 2, F])
        am = sb("am", [P, 2, F])
        aT = sb("aT", [P, 2, FC, P])
        yrow = sb("yrow", [P, 2, D])

        picked = XN[:].rearrange("p i d -> p (i d)")[:, 0:GS * K * D].rearrange("p (s k d) -> p s k d", s=GS, k=K)

        psT = pb("psT", [P, 512])
        psL = pb("psL", [P, 512])
        psG = [pb(f"psG{i}", [P, 512]) for i in range(2)]
        psV = [pb(f"psV{i}", [P, 512]) for i in range(2)]
        psAT = pb("psAT", [P, 512])
        psY = pb("psY", [P, 512])

        r_in = sem("r_in")
        w_in = sem("w_in2")
        ones_set = sem("ones_set2")
        stats3 = sem("stats3")
        var3_ready = sem("var3_ready")
        rstd_ready = sem("rstd_ready")
        xb_ready = sem("xb_ready")
        xb_mm = sem("xb_mm")
        xbT_ready = sem("xbT_ready")
        lg_mm = sem("lg_mm")
        kept_xn = sem("kept_xn")
        gap_ready = sem("gap_ready")
        exp_ready = sem("exp_ready")
        both_ready = sem("both_ready")
        rank_mm = sem("rank_mm")
        pos_ready = sem("pos_ready")
        te_ready = sem("te_ready")
        scattered = sem("scattered")
        dve_chain = sem("dve_chain2")
        pool_chain = sem("pool_chain2")
        xrow_in = [sem("xrow_in0"), sem("xrow_in1")]
        tx_mm = sem("tx_mm")
        xT_ready = sem("xT_ready")
        h_mm = sem("h_mm")
        silu_done = sem("silu_done")
        act_ready = sem("act_ready")
        at_mm = sem("at_mm")
        aT_ready = sem("aT_ready")
        y_mm = sem("y_mm")
        y_ready = sem("y_ready")
        y_out = [sem("y_out0"), sem("y_out1")]
        picked_in = [sem(f"picked_in{s}") for s in range(GS)]
        summed = sem("summed")
        row_out = [sem(f"row_out{s}") for s in range(GS)]

        block = ctx.enter_context(nc.Block())

        @block.sync
        def _(sp):
            for dst, src in ((wr, WrT), (tri, tri_d), (rev, rev_d), (tid, tid_d)):
                sp.dma_start(dst[:], src).then_inc(r_in, 16)
            for e in range(E):
                sp.dma_start(w1[:, e], W1T[:, e]).then_inc(w_in, 16)
                sp.dma_start(w2[:, e], W2T[:, e]).then_inc(w_in, 16)
            sp.wait_ge(scattered, 16 * K * TILES)

            def load(t, par):
                sp.dma_start(xrow[:, par], xs[bass.ds(t * P, P), :]).then_inc(xrow_in[par], 16)

            def store(t, par):
                sp.wait_ge(y_ready, t + 1)
                sp.dma_start(ys[bass.ds(t * P, P), :], yrow[:, par]).then_inc(y_out[par], 16)

            load(0, 0)
            load(1, 1)
            with sp.Fori(0, NS // 2 - 1) as j:
                for par in range(2):
                    sp.wait_ge(tx_mm, 2 * j + par + 1)
                    load(2 * j + par + 2, par)
                    store(2 * j + par, par)
            store(NS - 2, 0)
            store(NS - 1, 1)
            with sp.Fori(0, TILES // GS) as j:
                for s in range(GS):
                    sp.wait_ge(summed, GS * j + s + 1)
                    sp.dma_start(out[bass.ds((GS * j + s) * P, P), :], picked[:, s, 0, :]).then_inc(row_out[s], 16)
            for s in range(GS):
                sp.wait_ge(row_out[s], 16 * (TILES // GS))

        @block.gpsimd
        def _(pool):
            chain = Chain(pool, pool_chain)
            pool.wait_ge(var3_ready, 1)
            chain.done(pool.tensor_scalar(ve3[:], var3[:], EPS, None, ALU.add))
            pool.tensor_tensor(rstd3[:], ve3[:], mhalf[:].to_broadcast([P, TILES]), ALU.pow).then_inc(rstd_ready, 1)
            with pool.Fori(0, TILES // 2) as j:
                for par in range(2):
                    pool.wait_ge(xb_ready, 2 * j + par + 1)
                    pool.tensor_copy(XN[:, bass.ds(2 * j + par, 1), :].rearrange("p a d -> p (a d)"),
                                     xb[:, par]).then_inc(kept_xn, 1)
            pool.wait_ge(kept_xn, TILES)
            pool.wait_ge(pos_ready, 1)
            for i in range(TILES):
                for k in range(K):
                    pool.indirect_dma_start(xs, bass.IndirectOffsetOnAxis(ap=pos[:, k, i:i + 1], axis=0),
                                            XN[:, i, :], None).then_inc(scattered, 16)
            for par in range(2):
                pool.wait_ge(y_out[par], 16 * (NS // 2))
            for i in range(TILES):
                s = i % GS
                if i >= GS:
                    pool.wait_ge(row_out[s], 16 * (i // GS))
                for k in range(K):
                    pool.indirect_dma_start(picked[:, s, k, :], None, ys,
                                            bass.IndirectOffsetOnAxis(ap=pos[:, k, i:i + 1], axis=0)
                                            ).then_inc(picked_in[s], 16)

        @block.scalar
        def _(act):
            with act.Fori(0, TILES // 2) as j:
                for par in range(2):
                    act.wait_ge(xb_mm, 2 * j + par + 1)
                    act.activation(xbT[:, par], psT[:, 0:D].rearrange("p (c n) -> p c n", c=2),
                                   ACT.Identity).then_inc(xbT_ready, 1)
            act.wait_ge(gap_ready, 1)
            act.activation(egap[:], gap[:], ACT.Exp).then_inc(exp_ready, 1)

            def rows(t, par, head):
                act.wait_ge(tx_mm, t + 1)
                if not head:
                    act.wait_ge(h_mm, 2 * (t - 1))
                act.activation(xsT[:, par], psT[:, 0:D].rearrange("p (c n) -> p c n", c=2),
                               ACT.Identity).then_inc(xT_ready, 1)

            def silu(t, par, head):
                act.wait_ge(h_mm, 2 * t + 1)
                if not head:
                    act.wait_ge(act_ready, t - 1)
                act.activation(sg[:, par], psG[par][:, :], ACT.Silu).then_inc(silu_done, 1)

            def hidden(t, par, head):
                act.wait_ge(at_mm, t + 1)
                if not head:
                    act.wait_ge(y_mm, t - 1)
                act.activation(aT[:, par], psAT[:, :].rearrange("p (c n) -> p c n", c=FC),
                               ACT.Identity).then_inc(aT_ready, 1)

            def body(t, par, first, last):
                if not last:
                    rows(t + 1, 1 - par, first)
                if not first:
                    hidden(t - 1, 1 - par, False)
                silu(t, par, False)

            rows(0, 0, True)
            rows(1, 1, True)
            silu(0, 0, True)
            rows(2, 0, False)
            hidden(0, 0, True)
            silu(1, 1, True)
            rows(3, 1, False)
            hidden(1, 1, True)
            silu(2, 0, False)
            with act.Fori(0, (NS - 4) // 2) as j:
                body(2 * j + 3, 1, False, False)
                body(2 * j + 4, 0, False, False)
            body(NS - 1, 1, False, True)
            hidden(NS - 1, 1, False)

        @block.vector
        def _(dve):
            chain = Chain(dve, dve_chain)
            dve.memset(ones[:], 1.0).then_inc(ones_set, 1)
            with dve.Fori(0, TILES // 2) as j:
                for par in range(2):
                    i = 2 * j + par
                    xi = X[:, bass.ds(i, 1), :].rearrange("p a d -> p (a d)")
                    dve.bn_stats(st3[:, bass.ds(i, 1), :].rearrange("p a d -> p (a d)"), xi).then_inc(stats3, 1)
            dve.wait_ge(stats3, TILES)
            dve.tensor_tensor(mean3[:], st3[:, :, 1], st3[:, :, 4], ALU.add)
            dve.tensor_tensor(sq3[:], st3[:, :, 2], st3[:, :, 5], ALU.add)
            chain.done(dve.tensor_tensor(half3[:], st3[:, :, 1], st3[:, :, 4], ALU.subtract))
            dve.tensor_tensor(half3[:], half3[:], half3[:], ALU.mult)
            chain.done(dve.tensor_scalar(mean3[:], mean3[:], 0.5, None, ALU.mult))
            chain.done(dve.tensor_scalar(half3[:], half3[:], 0.25, None, ALU.mult))
            dve.scalar_tensor_tensor(var3[:], sq3[:], 1.0 / D, half3[:], ALU.mult, ALU.add).then_inc(var3_ready, 1)
            dve.wait_ge(rstd_ready, 1)

            def norm(i, par, head):
                if not head:
                    dve.wait_ge(xb_mm, i - 1)
                    dve.wait_ge(kept_xn, i - 1)
                dve.tensor_scalar(xb[:, par], X[:, bass.ds(i, 1), :].rearrange("p a d -> p (a d)"),
                                  mean3[:, bass.ds(i, 1)],
                                  rstd3[:, bass.ds(i, 1)], ALU.subtract, ALU.mult).then_inc(xb_ready, 1)

            norm(0, 0, True)
            norm(1, 1, True)
            with dve.Fori(0, TILES // 2 - 1) as j:
                norm(2 * j + 2, 0, False)
                norm(2 * j + 3, 1, False)
            dve.wait_ge(r_in, 16 * 4)

            dve.wait_ge(lg_mm, TILES)
            chain.done(dve.tensor_copy(lg[:], psL[:, 0:TILES * E].rearrange("p (i e) -> p i e", e=E)))
            rv = rev[:].unsqueeze(1).to_broadcast([P, TILES, E])
            cur = lg
            for k in range(K):
                chain.done(dve.reduce_max(top[:, k], cur[:], AX_X))
                chain.done(dve.tensor_tensor(eq[:], cur[:], top[:, k].unsqueeze(2).to_broadcast([P, TILES, E]),
                                             ALU.is_equal))
                chain.done(dve.tensor_tensor(eq[:], eq[:], rv, ALU.mult))
                chain.done(dve.reduce_max(first[:, k], eq[:], AX_X))
                chain.done(dve.tensor_tensor(hot[:, k], rv, first[:, k].unsqueeze(2).to_broadcast([P, TILES, E]),
                                             ALU.is_equal))
                if k == 0:
                    chain.done(dve.scalar_tensor_tensor(lm[:], hot[:, 0], -3e38, lg[:], ALU.mult, ALU.add))
                    cur = lm
            dve.tensor_tensor(gap[:], top[:, 1], top[:, 0], ALU.subtract).then_inc(gap_ready, 1)
            dve.tensor_tensor(both[:], hot[:, 0], hot[:, 1], ALU.add).then_inc(both_ready, 1)
            dve.wait_ge(exp_ready, 1)
            chain.done(dve.tensor_scalar(gap[:], egap[:], 1.0, None, ALU.add))
            chain.done(dve.reciprocal(wgt[:, 0], gap[:]))
            chain.done(dve.tensor_tensor(wgt[:, 1], egap[:], wgt[:, 0], ALU.mult))

            dve.wait_ge(rank_mm, 1)
            chain.done(dve.tensor_copy(tot[:], psG[0][:, TILES * E:2 * TILES * E].rearrange("p (i e) -> p i e", e=E)))
            chain.done(dve.tensor_copy(scan[:, 0], tot[:]))
            a, s = 0, 1
            while s < TILES:
                dve.tensor_copy(scan[:, 1 - a, 0:s], scan[:, a, 0:s])
                chain.done(dve.tensor_tensor(scan[:, 1 - a, s:TILES], scan[:, a, s:TILES],
                                             scan[:, a, 0:TILES - s], ALU.add))
                a, s = 1 - a, 2 * s
            chain.done(dve.tensor_scalar(cnt_i[:], scan[:, a, TILES - 1], float(P - 1), None, ALU.add))
            chain.done(dve.tensor_scalar(cnt_t[:], cnt_i[:], 7, None, ALU.logical_shift_right))
            chain.done(dve.tensor_copy(nt[:], cnt_t[:]))
            chain.done(dve.tensor_copy(escan[:, 0], nt[:]))
            b, s = 0, 1
            while s < E:
                dve.tensor_copy(escan[:, 1 - b, 0:s], escan[:, b, 0:s])
                chain.done(dve.tensor_tensor(escan[:, 1 - b, s:E], escan[:, b, s:E], escan[:, b, 0:E - s], ALU.add))
                b, s = 1 - b, 2 * s
            chain.done(dve.tensor_tensor(base[:], escan[:, b], nt[:], ALU.subtract))
            chain.done(dve.tensor_scalar(base[:], base[:], float(P), None, ALU.mult))
            chain.done(dve.tensor_tensor(posE[:], scan[:, a], tot[:], ALU.subtract))
            chain.done(dve.tensor_tensor(posE[:], posE[:],
                                         psG[0][:, 0:TILES * E].rearrange("p (i e) -> p i e", e=E), ALU.add))
            chain.done(dve.tensor_tensor(posE[:], posE[:], base[:].unsqueeze(1).to_broadcast([P, TILES, E]), ALU.add))
            for k in range(K):
                chain.done(dve.tensor_tensor(eq[:], hot[:, k], posE[:], ALU.mult))
                chain.done(dve.reduce_sum(posf[:, k], eq[:], AX_X))
            dve.tensor_copy(pos[:], posf[:]).then_inc(pos_ready, 1)
            chain.done(dve.tensor_tensor(past[:], tid[:].unsqueeze(2).to_broadcast([1, NS, E]),
                                         escan[0:1, b].unsqueeze(1).to_broadcast([1, NS, E]), ALU.is_ge))
            chain.done(dve.reduce_sum(tef[:], past[:], AX_X))
            dve.tensor_scalar(te[:], tef[:], float(E - 1), None, ALU.min).then_inc(te_ready, 1)

            def gate(t, par, head):
                dve.wait_ge(silu_done, t + 1)
                dve.wait_ge(h_mm, 2 * t + 2)
                if not head:
                    dve.wait_ge(at_mm, t - 1)
                dve.tensor_tensor(am[:, par], psV[par][:, :], sg[:, par], ALU.mult).then_inc(act_ready, 1)

            def result(t, par, j1, head):
                dve.wait_ge(y_mm, t + 1)
                if not head:
                    dve.wait_ge(y_out[par], j1)
                dve.tensor_copy(yrow[:, par], psY[:, 0:D]).then_inc(y_ready, 1)

            gate(0, 0, True)
            gate(1, 1, True)
            result(0, 0, 0, True)
            gate(2, 0, False)
            result(1, 1, 0, True)
            with dve.Fori(0, (NS - 4) // 2) as j:
                gate(2 * j + 3, 1, False)
                result(2 * j + 2, 0, 16 * (j + 1), False)
                gate(2 * j + 4, 0, False)
                result(2 * j + 3, 1, 16 * (j + 1), False)
            gate(NS - 1, 1, False)
            result(NS - 2, 0, 16 * (NS // 2 - 1), False)
            result(NS - 1, 1, 16 * (NS // 2 - 1), False)
            links = chain.n + chain.base
            with dve.Fori(0, TILES // GS) as j:
                chain.n, chain.base = 0, links + GS * j
                for s in range(GS):
                    i = GS * j + s
                    dve.wait_ge(picked_in[s], 16 * K * (j + 1))
                    acc = picked[:, s, 0, :]
                    xi = X[:, bass.ds(i, 1), :].rearrange("p a d -> p (a d)")
                    chain.done(dve.scalar_tensor_tensor(acc, acc, wgt[:, 0, bass.ds(i, 1)], xi, ALU.mult, ALU.add))
                    dve.scalar_tensor_tensor(acc, picked[:, s, 1, :], wgt[:, 1, bass.ds(i, 1)], acc, ALU.mult,
                                             ALU.add).then_inc(summed, 1)

        @block.tensor
        def _(pe):
            pe.wait_ge(r_in, 16 * 4)
            pe.wait_ge(ones_set, 1)

            def rowsT(i, par, head):
                pe.wait_ge(xb_ready, i + 1)
                if not head:
                    pe.wait_ge(xbT_ready, i)
                for c in range(2):
                    mm = pe.transpose(psT[:, c * P:(c + 1) * P], xb[:, par, c * P:(c + 1) * P], ident[:])
                mm.then_inc(xb_mm, 1)

            def logits(i, par):
                pe.wait_ge(xbT_ready, i + 1)
                for c in range(2):
                    mm = pe.matmul(psL[:, bass.ds(i * E, E)], xbT[:, par, c, :], wr[:, c, :], start=(c == 0),
                                   stop=(c == 1))
                mm.then_inc(lg_mm, 1)

            rowsT(0, 0, True)
            logits(0, 0)
            rowsT(1, 1, False)
            logits(1, 1)
            with pe.Fori(0, TILES // 2 - 1) as j:
                for par in range(2):
                    rowsT(2 * j + 2 + par, par, False)
                    logits(2 * j + 2 + par, par)
            pe.wait_ge(both_ready, 1)
            bv = both[:].rearrange("p i e -> p (i e)")
            pe.matmul(psG[0][:, 0:TILES * E], tri[:], bv, start=True, stop=True)
            pe.matmul(psG[0][:, TILES * E:2 * TILES * E], ones[:], bv, start=True, stop=True).then_inc(rank_mm, 1)
            pe.wait_ge(te_ready, 1)
            pe.wait_ge(w_in, 16 * 2 * E)

            def rows(t, par, j1, head):
                pe.wait_ge(xrow_in[par], j1)
                if not head:
                    pe.wait_ge(xT_ready, t)
                for c in range(2):
                    mm = pe.transpose(psT[:, c * P:(c + 1) * P], xrow[:, par, c * P:(c + 1) * P], ident[:])
                mm.then_inc(tx_mm, 1)

            def up(t, par, e, head):
                pe.wait_ge(xT_ready, t + 1)
                if not head:
                    pe.wait_ge(act_ready, t - 1)
                for bank, o in ((psG[par], F), (psV[par], 0)):
                    for c in range(2):
                        mm = pe.matmul(bank[:, :], xsT[:, par, c, :], w1[:, bass.ds(e, 1), c, o:o + F],
                                       start=(c == 0), stop=(c == 1))
                    mm.then_inc(h_mm, 1)

            def turn(t, par, head):
                pe.wait_ge(act_ready, t + 1)
                if not head:
                    pe.wait_ge(aT_ready, t)
                for c in range(FC):
                    mm = pe.transpose(psAT[:, c * P:(c + 1) * P], am[:, par, c * P:(c + 1) * P], ident[:])
                mm.then_inc(at_mm, 1)

            def down(t, par, e, head):
                pe.wait_ge(aT_ready, t + 1)
                if not head:
                    pe.wait_ge(y_ready, t)
                for c in range(FC):
                    mm = pe.matmul(psY[:, 0:D], aT[:, par, c, :], w2[:, bass.ds(e, 1), c, :],
                                   start=(c == 0), stop=(c == FC - 1))
                mm.then_inc(y_mm, 1)

            def expert(t):
                return pe.value_load(te[0:1, bass.ds(t, 1)], min_val=0, max_val=E - 1)

            rows(0, 0, 16, True)
            rows(1, 1, 16, False)
            up(0, 0, expert(0), True)
            rows(2, 0, 32, False)
            turn(0, 0, True)
            up(1, 1, expert(1), True)
            down(0, 0, expert(0), True)
            rows(3, 1, 32, False)
            turn(1, 1, False)
            up(2, 0, expert(2), False)
            down(1, 1, expert(1), False)
            with pe.Fori(0, (NS - 4) // 2) as j:
                for par in range(2):
                    t = 2 * j + 3 + par
                    rows(t + 1, par, 16 * (j + 3), False)
                    turn(t - 1, par, False)
                    up(t, 1 - par, expert(t), False)
                    down(t - 1, par, expert(t - 1), False)
            turn(NS - 2, 0, False)
            up(NS - 1, 1, expert(NS - 1), False)
            down(NS - 2, 0, expert(NS - 2), False)
            turn(NS - 1, 1, False)
            down(NS - 1, 1, expert(NS - 1), False)



def kernel(x, ctx_512, L0_xattn_Wq, L0_xattn_bq, L0_xattn_Wk, L0_xattn_bk, L0_xattn_Wv, L0_xattn_bv, L0_xattn_Wo,
           L0_xattn_bo, L0_attn_W_qkv, L0_attn_W_out, L0_attn_b_out, L0_ffn_Wr, L0_ffn_W1, L0_ffn_W2):
    import numpy as np
    import concourse.bacc as bacc
    from concourse.bass_utils import run_bass_kernel_spmd

    x = np.asarray(x)
    B = x.shape[0]
    tiles = B * Q // P

    def rows(w):
        return np.asarray(w).reshape(-1, P, w.shape[-1]).transpose(1, 0, 2)

    def spread(b):
        return np.broadcast_to(np.asarray(b), (P, D))

    pos = np.arange(P) % Q
    ang = pos[:, None].astype(np.float32) * (1.0 / 10000.0 ** (np.arange(DH // 2, dtype=np.float32) / (DH // 2)))
    ang = ang.astype(np.float32)
    cos, sin = np.cos(ang), np.sin(ang)
    arrays = {
        "x": x.reshape(tiles, P, D).transpose(1, 0, 2),
        "ctxT": np.asarray(ctx_512).transpose(2, 0, 1).reshape(CD, -1),
        "Wq": rows(L0_xattn_Wq),
        "bq": np.asarray(L0_xattn_bq).reshape(2, P).T,
        "Wk": np.asarray(L0_xattn_Wk),
        "bk": np.asarray(L0_xattn_bk).reshape(2, P).T,
        "Wv": np.asarray(L0_xattn_Wv),
        "bvT": np.asarray(L0_xattn_bv).reshape(4, 4, DH).transpose(0, 2, 1).reshape(4 * DH, 4),
        "WoR": np.asarray(L0_xattn_Wo).reshape(4, 4, DH, D).transpose(0, 2, 1, 3).reshape(4 * DH, 4, D),
        "bo": spread(L0_xattn_bo),
        "Wqkv": rows(L0_attn_W_qkv),
        "Wout": rows(L0_attn_W_out),
        "bout": spread(L0_attn_b_out),
        "ident": np.eye(P, dtype=np.float32),
        "hmask": (np.arange(P)[:, None] // DH == np.arange(HC)[None]).astype(np.float32),
        "cos": np.stack([cos, cos], -1).reshape(P, DH),
        "sin": np.stack([-sin, sin], -1).reshape(P, DH),
        "causal": np.where(np.arange(Q)[None] <= pos[:, None], 0, -1e9 * DH ** 0.5).astype(np.float32),
        "WrT": np.asarray(L0_ffn_Wr).T.reshape(2, P, E).transpose(1, 0, 2),
        "W1T": np.asarray(L0_ffn_W1).transpose(2, 0, 1).reshape(2, P, E, 2 * F).transpose(1, 2, 0, 3),
        "W2T": np.asarray(L0_ffn_W2).transpose(2, 0, 1).reshape(F // P, P, E, D).transpose(1, 2, 0, 3),
        "tri": np.triu(np.ones((P, P), np.float32), 1),
        "rev": np.broadcast_to(E - np.arange(E, dtype=np.float32), (P, E)),
        "tid": np.arange(SLOT_TILES(tiles), dtype=np.float32)[None],
    }
    arrays = {f"in_{k}": np.ascontiguousarray(v) for k, v in arrays.items()}
    nc = bacc.Bacc("TRN2", target_bir_lowering=False, num_devices=1)
    args = [nc.dram_tensor(k, v.shape, mybir.dt.from_np(v.dtype), kind="ExternalInput").ap()
            for k, v in arrays.items()]
    out = nc.dram_tensor("out", (tiles * P, D), F32, kind="ExternalOutput").ap()
    perceiver(nc, *args, out)
    r = run_bass_kernel_spmd(nc, [arrays], core_ids=[0])
    return r.results[0]["out"].reshape(B, Q, D)
```

```python
from contextlib import ExitStack

import concourse.bass as bass
from concourse import mybir

F32 = mybir.dt.float32
F32R = mybir.dt.float32r
I32 = mybir.dt.int32
U32 = mybir.dt.uint32
ALU = mybir.AluOpType
ACT = mybir.ActivationFunctionType
AX_X = mybir.AxisListType.X

P = 128
Q = 32
D = 256
CD = 128
KV = 257
H = 16
DH = D // H
BT = P // Q
HC = H // 2
KT = 2
EPS = 1e-5
E = 8
F = 512
K = 2
DVE_LINKS = 24
POOL_LINKS = 4


def SLOT_TILES(tiles):
    return K * tiles + E


class Chain:

    def __init__(self, eng, sem):
        self.eng, self.sem, self.base, self.n = eng, sem, 0, 0

    def done(self, ins, wait=None):
        self.n += 1
        ins.then_inc(self.sem, 1)
        if wait:
            wait(self.eng, self.sem, self.base + self.n)
        else:
            self.eng.wait_ge(self.sem, self.base + self.n)


def perceiver(nc, x, ctxT, Wq, bq, Wk, bk, Wv, bvT, WoR, bo, Wqkv, Wout, bout, ident_d, hmask_d, cos_d, sin_d,
              causal_d, fold_d, hsel_d, chead_d, WrT, W1T, W2T, tri_d, rev_d, tid_d, out):
    TILES = x.shape[1]
    assert TILES % 2 == 0 and TILES >= 6

    xs = nc.dram_tensor("slot_rows", (SLOT_TILES(TILES) * P, D), F32, kind="Internal").ap()
    ys = nc.dram_tensor("slot_outputs", (SLOT_TILES(TILES) * P, D), F32, kind="Internal").ap()

    with ExitStack() as whole:
        def kept(name, shape, dt=F32):
            return whole.enter_context(nc.sbuf_tensor(name, shape, dt))

        X = kept("X", [P, TILES, D])
        ident = kept("ident", [P, P])
        mhalf = kept("mhalf", [P, 1])
        attentions(nc, X, ident, mhalf, xs, x, ctxT, Wq, bq, Wk, bk, Wv, bvT, WoR, bo, Wqkv, Wout, bout, ident_d,
                   hmask_d, cos_d, sin_d, causal_d, fold_d, hsel_d, chead_d)
        experts(nc, X, ident, mhalf, xs, ys, WrT, W1T, W2T, tri_d, rev_d, tid_d, out)


def attentions(nc, X, ident, mhalf, xs, x, ctxT, Wq, bq, Wk, bk, Wv, bvT, WoR, bo, Wqkv, Wout, bout, ident_d,
               hmask_d, cos_d, sin_d, causal_d, fold_d, hsel_d, chead_d):
    TILES = X.shape[1]
    LAST = TILES - 1
    CW = BT * KV

    with ExitStack() as ctx:
        def sb(name, shape, dt=F32):
            return ctx.enter_context(nc.sbuf_tensor(name, shape, dt))

        def pb(name, shape, dt=F32):
            return ctx.enter_context(nc.psum_tensor(name, shape, dt))

        def sem(name):
            return ctx.enter_context(nc.semaphore(name))

        zeros = sb("zeros", [P, 8, D])
        cT = sb("cT", [P, 2, CW])
        wq = sb("wq", [P, 2, D])
        wk = sb("wk", [P, D])
        wv = sb("wv", [P, D])
        wo = sb("wo", [64, 4, D])
        wqkv = sb("wqkv", [P, 2, 3 * D])
        wout = sb("wout", [P, 2, D])
        bq_s = sb("bq_s", [P, 2])
        bk_s = sb("bk_s", [P, 2])
        bv_s = sb("bv_s", [64, 4])
        bo_s = sb("bo_s", [P, D])
        bout_s = sb("bout_s", [P, D])
        hmask = sb("hmask", [P, HC])
        cos_s = sb("cos_s", [P, DH])
        sin_s = sb("sin_s", [P, DH])
        causal = sb("causal", [P, Q])
        causal_r = sb("causal_r", [P, Q], F32R)
        ident_r = sb("ident_r", [P, P], F32R)
        neg1 = sb("neg1", [P, P], F32R)
        stat = sb("stat", [P, 2, 6])
        mv = sb("mv", [P, 2, 2])
        rstd = sb("rstd", [P, 2])
        vareps = sb("vareps", [P, 2])
        xn1 = sb("xn1", [P, D])
        xT1 = sb("xT1", [P, 2, P])
        qT = sb("qT", [P, 2, 2, P])
        qblk = sb("qblk", [P, 2, 2, HC, Q])
        qblk_r = sb("qblk_r", [P, 2, 2, HC, Q], F32R)
        kT = sb("kT", [P, 2, 2, KV])
        kT_r = sb("kT_r", [P, 2, 2, KV + 1], F32R)
        vS = sb("vS", [P, 2, KT, H, DH + 1])
        kblk = sb("kblk", [P, 2, 2 * (Q + HC)])
        vblk = sb("vblk", [P, H, DH + 1])
        mblk = sb("mblk", [P, 2, Q], F32R)
        pL = sb("pL", [P, Q])
        fold = sb("fold", [P, Q])
        hsel = sb("hsel", [P, H])
        chead = sb("chead", [P, BT])
        mx = sb("mx", [P, 2, 4])
        mdiag = sb("mdiag", [P, 2, 4, P], F32R)
        pT = sb("pT", [P, 2, KT, H * Q])
        rs = sb("rs", [P, BT, 4])
        on = sb("on", [P, BT, 4, DH])
        oT = sb("oT", [64, 4, BT, Q])
        tmp = sb("tmp", [P, D])
        xn2 = sb("xn2", [P, D])
        xT2 = sb("xT2", [P, 2, P])
        rot = sb("rot", [P, 2 * D])
        swp = sb("swp", [P, 2 * D])
        v2 = sb("v2", [P, H, DH + 1])
        qkT = sb("qkT", [P, 4, P])
        qblk2 = sb("qblk2", [P, 2, BT, HC, Q])
        s2 = sb("s2", [P, H, Q])
        m2 = sb("m2", [P, H])
        r2 = sb("r2", [P, H])
        pT2 = sb("pT2", [P, H * Q])
        o2 = sb("o2", [P, D])
        o2T = sb("o2T", [P, 2, P])

        psP = [pb(f"psP{i}", [P, 512]) for i in range(2)]
        psA = [pb(f"psA{i}", [P, 512]) for i in range(2)]
        psB = [pb(f"psB{i}", [P, 512]) for i in range(2)]
        psO = pb("psO", [P, 512])
        psX = pb("psX", [P, 512])
        oV = psO[:, 0:BT * 4 * (DH + 1)].rearrange("p (b g d) -> p b g d", b=BT, g=4)

        x_in = [sem("x_in0"), sem("x_in1")]
        w_in = sem("w_in")
        ctx_in = [sem("ctx_in0"), sem("ctx_in1")]
        ones_set = sem("ones_set")
        zeros_set = sem("zeros_set")
        mask_ready = sem("mask_ready")
        k_mm = sem("k_mm")
        k_ev = sem("k_ev")
        kr_ready = sem("kr_ready")
        kblk_ready = sem("kblk_ready")
        qr_ready = sem("qr_ready")
        v_mm = sem("v_mm")
        v_ev = sem("v_ev")
        a_mm = sem("a_mm")
        max_done = sem("max_done")
        d_ready = sem("d_ready")
        sb_mm = sem("sb_mm")
        exp_done = sem("exp_done")
        pv_mm = sem("pv_mm")
        on_ready = sem("on_ready")
        q_ready = sem("q_ready")
        qblk_ready = sem("qblk_ready")
        var1 = sem("var1")
        var2 = sem("var2")
        rstd1 = sem("rstd1")
        rstd2 = sem("rstd2")
        ln1 = sem("ln1")
        step_mm = sem("step_mm")
        step_ready = sem("step_ready")
        tr_copied = sem("tr_copied")
        sub_done = sem("sub_done")
        exp2_done = sem("exp2_done")
        dve_chain = sem("dve_chain")
        pool_chain = sem("pool_chain")
        carried = sem("carried")
        x_out = sem("x_out")
        N_W = 19
        N_SET = 6

        def wait_apart(eng, semaphore, value):
            eng.wait_ge(semaphore, value)
            if not isinstance(value, int):
                eng.sem_inc(carried, 1)

        STEPS = ((8, "P0", "P1", 0), (9, 1, None, 2), (None, 3, 4, 5), (None, None, 6, 7))
        ORDER = [s for row in STEPS for s in row if s is not None]

        def lag(s):
            return 2 if s in (8, 9) else 1

        def steps_of(tau, first, last):
            if first:
                return ["P0", "P1"]
            return [s for s in ORDER if not (last and isinstance(s, str)) and not (
                isinstance(tau, int) and tau == 1 and s in (8, 9))]

        def step_at(tau, b, where, first, last):
            s = STEPS[b][where]
            mine = steps_of(tau, first, last)
            if s is None or s not in mine:
                return None
            if first:
                return s, 2 + mine.index(s)
            if isinstance(tau, int) and tau == 1:
                return s, 4 + mine.index(s)
            return s, 14 + (tau - 2) * 12 + mine.index(s)

        def final_steps():
            n = 14 + (LAST - 2) * 12 + 10
            return [(8, LAST - 1, n), (9, LAST - 1, n + 1)] + [(e, LAST, n + 2 + e) for e in range(10)]

        def ctx_wait(eng, tau, par):
            eng.wait_ge(ctx_in[par], (tau - par) * 8 + 16)

        def over_tiles(eng, body, chain=None, links=0):
            body(0, 0, True, False)
            body(1, 1, False, False)
            start = chain.n if chain else 0
            with eng.Fori(0, (TILES - 4) // 2) as j:
                if chain:
                    chain.base = j * links
                body(2 * j + 2, 0, False, False)
                body(2 * j + 3, 1, False, False)
            if chain:
                assert chain.n - start == links, chain.n - start
                chain.base = ((TILES - 4) // 2 - 1) * links
            body(LAST - 1, 0, False, False)
            body(LAST, 1, False, True)

        block = ctx.enter_context(nc.Block())

        @block.sync
        def _(sp):
            sp.dma_start(X[:, 0:1, :], x[:, 0:1, :]).then_inc(x_in[0], 16)
            for dst, src in ((ident, ident_d), (wq, Wq), (bq_s, bq), (hmask, hmask_d), (wk, Wk), (wv, Wv),
                             (bk_s, bk)):
                sp.dma_start(dst[:], src).then_inc(w_in, 16)

            def load_ctx(tau, par):
                sp.dma_start(cT[:, par, :], ctxT[:, bass.ds(tau * CW, CW)]).then_inc(ctx_in[par], 16)

            load_ctx(0, 0)
            load_ctx(1, 1)
            sp.dma_start(X[:, 1:TILES, :], x[:, 1:TILES, :]).then_inc(x_in[1], 16)
            for dst, src in ((wo, WoR), (bv_s, bvT), (bo_s, bo), (wqkv, Wqkv), (cos_s, cos_d), (sin_s, sin_d),
                             (causal, causal_d), (fold, fold_d), (hsel, hsel_d), (chead, chead_d), (wout, Wout), (bout_s, bout)):
                sp.dma_start(dst[:], src).then_inc(w_in, 16)
            with sp.Fori(0, (TILES - 2) // 2) as j:
                sp.wait_ge(v_mm, 16 * j + 8)
                load_ctx(2 * j + 2, 0)
                sp.wait_ge(v_mm, 16 * j + 16)
                load_ctx(2 * j + 3, 1)
            sp.wait_ge(zeros_set, 1)
            for r in range(0, SLOT_TILES(TILES), 8):
                n = min(8, SLOT_TILES(TILES) - r)
                sp.dma_start(xs[r * P:(r + n) * P, :].rearrange("(p r) d -> p r d", p=P),
                             zeros[:, 0:n, :]).then_inc(x_out, 16)
            sp.wait_ge(x_out, 16 * (-(-SLOT_TILES(TILES) // 8)))

        @block.gpsimd
        def _(pool):
            chain = Chain(pool, pool_chain)
            chain.done(pool.memset(mhalf[:], -0.5))
            pool.wait_ge(w_in, 16 * N_W)

            def inv_std(k, tau, var, done):
                wait_apart(pool, var, tau + 1)
                chain.done(pool.tensor_scalar(vareps[:, k:k + 1], mv[:, k, 1:2], EPS, None, ALU.add))
                pool.tensor_tensor(rstd[:, k:k + 1], vareps[:, k:k + 1], mhalf[:], ALU.pow).then_inc(done, 1)

            def spread_q(tau, par, b):
                g = 4 * tau + b
                pool.wait_ge(q_ready, tau + 1)
                if not (isinstance(tau, int) and g < 2):
                    pool.wait_ge(sb_mm, 3 * (g - 1))
                src = qT[:, par, :, b * Q:(b + 1) * Q]
                pool.tensor_tensor(qblk[:, b % 2], src.unsqueeze(2).to_broadcast([P, 2, HC, Q]),
                                   hmask[:].unsqueeze(1).unsqueeze(3).to_broadcast([P, 2, HC, Q]),
                                   ALU.mult).then_inc(qblk_ready, 1)

            def spread_k(g, par_g):
                pool.wait_ge(k_ev, 2 * g + 2)
                dst = kblk[:, par_g].rearrange("p (c w) -> p c w", c=2)[:, :, 0:HC]
                pool.tensor_tensor(dst, kT[:, par_g, :, KV - 1:KV].to_broadcast([P, 2, HC]),
                                   hmask[:].unsqueeze(1).to_broadcast([P, 2, HC]), ALU.mult).then_inc(kblk_ready, 1)

            def spread_q2(n):
                pool.wait_ge(tr_copied, n)
                for c in range(2):
                    src = qkT[:, c, :].rearrange("p (b q) -> p b q", b=BT)
                    ins = pool.tensor_tensor(qblk2[:, c], src.unsqueeze(2).to_broadcast([P, BT, HC, Q]),
                                             hmask[:].unsqueeze(1).unsqueeze(3).to_broadcast([P, BT, HC, Q]),
                                             ALU.mult)
                ins.then_inc(step_ready, 1)

            def body(tau, par, first, last):
                for b in range(BT):
                    if b < 3:
                        spread_q(tau, par, b + 1)
                        spread_k(4 * tau + b + 1, (b + 1) % 2)
                    elif not last:
                        spread_q(tau + 1, 1 - par, 0)
                        spread_k(4 * tau + 4, 0)
                    if b == 2 and not (isinstance(tau, int) and tau + 2 > LAST):
                        inv_std(0, tau + 2, var1, rstd1)
                    if b == 2 and not first:
                        spread_q2(tau)
                    if b == 0 and not first:
                        inv_std(1, tau - 1, var2, rstd2)

            inv_std(0, 0, var1, rstd1)
            inv_std(0, 1, var1, rstd1)
            pool.wait_ge(ones_set, N_SET)
            spread_q(0, 0, 0)
            spread_k(0, 0)
            over_tiles(pool, body, chain, POOL_LINKS)
            inv_std(1, LAST, var2, rstd2)
            spread_q2(LAST + 1)

        @block.scalar
        def _(act):
            act.wait_ge(w_in, 16 * N_W)

            def step_copy(dst, src, n, sem2=None):
                act.wait_ge(step_mm, n + 1)
                ins = act.activation(dst, src, ACT.Identity)
                ins.then_inc(sem2 or step_ready, 1)

            def x2v(t):
                return psX[:, 0:2 * P].rearrange("p (c n) -> p c n", c=2)

            def keys(g, par_g, first=False):
                for c in range(2):
                    act.wait_ge(k_mm, 2 * g + c + 1)
                    if not first:
                        act.wait_ge(sb_mm, 3 * (g - 1))
                    act.activation(kT[:, par_g, c, :], psP[c][:, 0:KV], ACT.Identity,
                                   bias=bk_s[:, c:c + 1]).then_inc(k_ev, 1)
                act.wait_ge(k_ev, 2 * g + 2)
                if not first:
                    act.wait_ge(a_mm, 4 * (g - 1))
                act.activation(kT_r[:, par_g, :, 0:KV], kT[:, par_g], ACT.Identity).then_inc(kr_ready, 1)

            def exps(g, par_g, b, first=False):
                for t in range(KT):
                    act.wait_ge(sb_mm, 3 * g + t + 1)
                    if not first:
                        act.wait_ge(pv_mm, g - 1)
                    act.activation(pT[:, par_g, t, :], psB[(3 * par_g + t) % 2][:, :], ACT.Exp).then_inc(exp_done, 1)
                act.wait_ge(sb_mm, 3 * g + 3)
                s = slice(b * Q, (b + 1) * Q)
                act.activation(pL[s, :], psB[par_g % 2][s, 0:Q], ACT.Exp).then_inc(exp_done, 1)

            def slot(tau, b, where, first, last):
                at = step_at(tau, b, where, first, last)
                if not at:
                    return
                s, n = at
                if s == "P0":
                    step_copy(xT1[:], x2v(0), n)
                elif s != "P1":
                    epi(tau - lag(s), s, n)

            def epi(tau, e, n):
                if e == 2:
                    step_copy(xT2[:], x2v(0), n)
                elif e == 4:
                    step_copy(v2[:, :, 0:DH], psX[:, 0:D].rearrange("p (h d) -> p h d", h=H), n)
                elif e == 5:
                    step_copy(qkT[:], psX[:, :].rearrange("p (c n) -> p c n", c=4), n, tr_copied)
                elif e == 6:
                    act.wait_ge(sub_done, tau + 1)
                    act.activation(s2[:], s2[:], ACT.Exp, scale=DH ** -0.5).then_inc(exp2_done, 1)
                elif e == 8:
                    step_copy(o2T[:], x2v(0), n)

            def body(tau, par, first, last):
                for b in range(BT):
                    g = 4 * tau + b
                    slot(tau, b, 0, first, last)
                    if not (last and b == 3):
                        keys(g + 1, (b + 1) % 2, first=first and b == 0)
                    slot(tau, b, 1, first, last)
                    slot(tau, b, 2, first, last)
                    exps(g, b % 2, b, first=first and b < 2)
                    slot(tau, b, 3, first, last)

            step_copy(xT1[:], x2v(0), 0)
            keys(0, 0, first=True)
            over_tiles(act, body)
            for e, tau, n in final_steps():
                epi(tau, e, n)

        @block.vector
        def _(dve):
            chain = Chain(dve, dve_chain)
            dve.memset(neg1[:].bitcast(F32), -1.0).then_inc(ones_set, 1)
            dve.memset(kT_r[:].bitcast(F32)[:, :, :, KV:KV + 1], 0.0).then_inc(ones_set, 1)
            dve.memset(vS[:, :, :, :, DH:DH + 1], 1.0).then_inc(ones_set, 1)
            dve.memset(v2[:, :, DH:DH + 1], 1.0).then_inc(ones_set, 1)
            dve.memset(kblk[:], 0.0).then_inc(ones_set, 1)
            dve.memset(mblk[:].bitcast(F32), 0.0).then_inc(ones_set, 1)
            dve.memset(zeros[:], 0.0).then_inc(zeros_set, 1)
            dve.wait_ge(x_in[0], 16)

            def norm(k, tau, src, dst, var, rdy, done):
                chain.done(dve.bn_stats(stat[:, k], src), wait_apart)
                dve.bn_aggr(mv[:, k], stat[:, k]).then_inc(var, 1)
                dve.wait_ge(var, tau + 1)
                dve.wait_ge(rdy, tau + 1)
                dve.tensor_scalar(dst, src, mv[:, k, 0:1], rstd[:, k:k + 1], ALU.subtract, ALU.mult).then_inc(done, 1)

            def xi(tau):
                return X[:, bass.ds(tau, 1), :].rearrange("p a d -> p (a d)")

            def query(tau, par, n, first):
                dve.wait_ge(step_mm, n + 1)
                if not first:
                    dve.wait_ge(qblk_ready, 4 * (tau - 1))
                    dve.wait_ge(sb_mm, 12 * (tau - 1))
                chain.done(dve.tensor_tensor(qT[:, par], psX[:, 0:2 * P].rearrange("p (c n) -> p c n", c=2),
                                             bq_s[:].unsqueeze(2).to_broadcast([P, 2, P]), ALU.add))
                chain.done(dve.tensor_scalar(qT[:, par], qT[:, par], DH ** -0.5, None, ALU.mult))
                dve.sem_inc(q_ready, 1)
                dve.sem_inc(step_ready, 1)

            def values(g, par_g, b, first=False):
                dve.wait_ge(v_mm, 2 * g + 1)
                if not first:
                    dve.wait_ge(pv_mm, g - 1)
                dve.tensor_copy(vS[:, par_g, 0:2, :, 0:DH],
                                psP[0][:, :].rearrange("p (t h d) -> p t h d", t=2, h=H)).then_inc(v_ev, 1)
                dve.wait_ge(v_mm, 2 * g + 2)
                s = slice(b * Q, (b + 1) * Q)
                dve.tensor_tensor(vblk[s, :, 0:DH], psP[1][s, 0:D].rearrange("p (h d) -> p h d", h=H),
                                  hsel[s, :].unsqueeze(2).to_broadcast([Q, H, DH]), ALU.mult).then_inc(v_ev, 1)

            def round_q(g, par_g):
                dve.wait_ge(qblk_ready, g + 1)
                dve.tensor_copy(qblk_r[:, par_g], qblk[:, par_g]).then_inc(qr_ready, 1)

            def maxima(g, par_g, half, first=False):
                for a in (2 * half, 2 * half + 1):
                    dve.wait_ge(a_mm, 4 * g + a + 1)
                    dve.reduce_max(mx[:, par_g, a:a + 1], psA[a % 2][:, 0:KV], AX_X).then_inc(max_done, 1)
                if half == 0:
                    return
                dve.wait_ge(max_done, 4 * g + 4)
                if not first:
                    dve.wait_ge(sb_mm, 3 * (g - 1))
                dve.tensor_tensor(mdiag[:, par_g], ident[:].unsqueeze(1).to_broadcast([P, 4, P]),
                                  mx[:, par_g].unsqueeze(2).to_broadcast([P, 4, P]),
                                  ALU.mult).then_inc(d_ready, 1)
                dve.tensor_tensor(mblk[:, par_g, 0:H].rearrange("p (g c) -> p g c", c=BT),
                                  chead[:].unsqueeze(1).to_broadcast([P, 4, BT]),
                                  mx[:, par_g].unsqueeze(2).to_broadcast([P, 4, BT]), ALU.mult).then_inc(d_ready, 1)

            def norm_o(tau):
                dve.wait_ge(pv_mm, 4 * tau + 4)
                chain.done(dve.reciprocal(rs[:], oV[:, :, :, DH]))
                dve.tensor_tensor(on[:], oV[:, :, :, 0:DH], rs[:].unsqueeze(3).to_broadcast([P, BT, 4, DH]),
                                  ALU.mult).then_inc(on_ready, 1)

            def epi(tau, e, n):
                if e == 0:
                    dve.wait_ge(step_mm, n + 1)
                    dve.tensor_tensor(oT[:].rearrange("p c b q -> p b c q"),
                                      psX[0:64, :].rearrange("p (b c q) -> p b c q", b=BT, c=4),
                                      bv_s[:].unsqueeze(1).unsqueeze(3).to_broadcast([64, BT, 4, Q]),
                                      ALU.add).then_inc(step_ready, 1)
                elif e == 1:
                    dve.wait_ge(step_mm, n + 1)
                    chain.done(dve.tensor_tensor(tmp[:], psX[:, 0:D], bo_s[:], ALU.add))
                    chain.done(dve.tensor_tensor(xi(tau), xi(tau), tmp[:], ALU.add), wait_apart)
                    norm(1, tau, xi(tau), xn2[:], var2, rstd2, step_ready)
                elif e == 3:
                    dve.wait_ge(step_mm, n + 1)
                    ps = psX[:, :].rearrange("p (h f e) -> p h f e", f=DH // 2, e=2)
                    sv = swp[:].rearrange("p (h f e) -> p h f e", f=DH // 2, e=2)
                    sn = sin_s[:].rearrange("p (f e) -> p f e", e=2)
                    for e2 in range(2):
                        dve.tensor_tensor(sv[:, :, :, e2], ps[:, :, :, 1 - e2],
                                          sn[:, :, e2].unsqueeze(1).to_broadcast([P, 2 * H, DH // 2]), ALU.mult)
                    chain.done(dve.tensor_tensor(rot[:].rearrange("p (h d) -> p h d", d=DH),
                                                 psX[:, :].rearrange("p (h d) -> p h d", d=DH),
                                                 cos_s[:].unsqueeze(1).to_broadcast([P, 2 * H, DH]), ALU.mult))
                    dve.tensor_tensor(rot[:], rot[:], swp[:], ALU.add).then_inc(step_ready, 1)
                elif e == 6:
                    dve.wait_ge(step_mm, n + 1)
                    chain.done(dve.transpose(s2[:].rearrange("p h k -> p (h k)"), psX[:, :]))
                    chain.done(dve.reduce_max(m2[:], s2[:], AX_X))
                    dve.tensor_tensor(s2[:], s2[:], m2[:].unsqueeze(2).to_broadcast([P, H, Q]),
                                      ALU.subtract).then_inc(sub_done, 1)
                    dve.wait_ge(exp2_done, tau + 1)
                    dve.transpose(pT2[:], s2[:].rearrange("p h k -> p (h k)")).then_inc(step_ready, 1)
                elif e == 7:
                    dve.wait_ge(step_mm, n + 1)
                    ov = psX[:, 0:H * (DH + 1)].rearrange("p (h d) -> p h d", h=H)
                    chain.done(dve.reciprocal(r2[:], ov[:, :, DH]))
                    dve.tensor_tensor(o2[:].rearrange("p (h d) -> p h d", h=H), ov[:, :, 0:DH],
                                      r2[:].unsqueeze(2).to_broadcast([P, H, DH]), ALU.mult).then_inc(step_ready, 1)
                elif e == 9:
                    dve.wait_ge(step_mm, n + 1)
                    chain.done(dve.tensor_tensor(tmp[:], psX[:, 0:D], bout_s[:], ALU.add))
                    dve.tensor_tensor(xi(tau), xi(tau), tmp[:], ALU.add).then_inc(step_ready, 1)

            def slot(tau, par, b, where, first, last):
                at = step_at(tau, b, where, first, last)
                if not at:
                    return
                s, n = at
                if s == "P1":
                    query(tau + 1, 1 - par, n, first)
                elif s != "P0":
                    epi(tau - lag(s), s, n)

            def body(tau, par, first, last):
                for b in range(BT):
                    g = 4 * tau + b
                    maxima(g, b % 2, 0)
                    slot(tau, par, b, 0, first, last)
                    maxima(g, b % 2, 1, first=first and b < 2)
                    if b == 0 and not first:
                        norm_o(tau - 1)
                    slot(tau, par, b, 1, first, last)
                    if not (last and b == 3):
                        values(g + 1, (b + 1) % 2, (b + 1) % BT, first=first and b == 0)
                    slot(tau, par, b, 2, first, last)
                    if not (last and b == 3):
                        round_q(g + 1, (b + 1) % 2)
                    if b == 2 and not (isinstance(tau, int) and tau + 2 > LAST):
                        norm(0, tau + 2, xi(tau + 2), xn1[:], var1, rstd1, ln1)
                    slot(tau, par, b, 3, first, last)

            norm(0, 0, X[:, 0, :], xn1[:], var1, rstd1, ln1)
            dve.wait_ge(w_in, 16 * N_W)
            dve.tensor_copy(causal_r[:], causal[:]).then_inc(mask_ready, 1)
            dve.tensor_copy(ident_r[:], ident[:]).then_inc(mask_ready, 1)
            dve.tensor_copy(vblk[:, :, DH], hsel[:]).then_inc(mask_ready, 1)
            dve.wait_ge(x_in[1], 16)
            query(0, 0, 1, True)
            norm(0, 1, X[:, 1, :], xn1[:], var1, rstd1, ln1)
            values(0, 0, 0, first=True)
            round_q(0, 0)
            over_tiles(dve, body, chain, DVE_LINKS)
            norm_o(LAST)
            for e, tau, n in final_steps():
                epi(tau, e, n)

        @block.tensor
        def _(pe):
            pe.wait_ge(ones_set, N_SET)
            pe.wait_ge(mask_ready, 3)
            pe.wait_ge(w_in, 16 * N_W)

            def keys(tau, par, b, first=False):
                g = 4 * tau + b
                if b == 0:
                    ctx_wait(pe, tau, par)
                for c in range(2):
                    if not first:
                        pe.wait_ge(v_ev, 2 * g - 1 + c)
                    pe.matmul(psP[c][:, 0:KV], wk[:, c * P:(c + 1) * P], cT[:, par, b * KV:(b + 1) * KV],
                              start=True, stop=True).then_inc(k_mm, 1)

            def values(tau, par, b):
                g = 4 * tau + b
                pe.wait_ge(k_ev, 2 * g + 1)
                for t in range(2):
                    mm = pe.matmul(psP[0][:, t * D:(t + 1) * D], cT[:, par, b * KV + t * P:b * KV + (t + 1) * P],
                                   wv[:], start=True, stop=True)
                mm.then_inc(v_mm, 1)
                pe.wait_ge(k_ev, 2 * g + 2)
                pe.matmul(psP[1][b * Q:(b + 1) * Q, 0:D], cT[:, par, (b + 1) * KV - 1:(b + 1) * KV].to_broadcast([P, Q]),
                          wv[:], start=True, stop=True).then_inc(v_mm, 1)

            def score_rows(g, par_g, half, first=False):
                if half == 0:
                    pe.wait_ge(qr_ready, g + 1)
                    pe.wait_ge(kr_ready, g + 1)
                for a in (2 * half, 2 * half + 1):
                    if not (first and a < 2):
                        pe.wait_ge(max_done, 4 * g + a - 1)
                    pe.matmul(psA[a % 2][:, 0:KV + 1], qblk_r[:, par_g, a // 2, 4 * (a % 2):4 * (a % 2) + 4, :],
                              kT_r[:, par_g, a // 2, :], start=True, stop=True).then_inc(a_mm, 1)

            def score_cols(g, par_g, par, b, first=False):
                pe.wait_ge(d_ready, 2 * g + 1)
                pe.wait_ge(k_ev, 2 * g + 2)
                for t in range(KT):
                    bank = psB[(3 * par_g + t) % 2]
                    if not (first and t < 2):
                        pe.wait_ge(exp_done, 3 * g + t - 1)
                    pe.matmul(bank[:, :], neg1[:], mdiag[:, par_g], start=True, stop=False, skip_group_check=True)
                    for c in range(2):
                        mm = pe.matmul(bank[:, c * 256:(c + 1) * 256], kT[:, par_g, c, t * P:(t + 1) * P],
                                       qblk[:, par_g, c], start=False, stop=True, skip_group_check=True)
                    mm.then_inc(sb_mm, 1)
                wait_apart(pe, d_ready, 2 * g + 2)
                wait_apart(pe, kblk_ready, g + 1)
                wait_apart(pe, exp_done, 3 * g + 1)
                s = slice(b * Q, (b + 1) * Q)
                row = psB[par_g % 2][s, 0:Q]
                pe.matmul(row, mblk[:, par_g].bitcast(F32), fold[:], start=True, stop=False, skip_group_check=True)
                for c in range(2):
                    mm = pe.matmul(row, kblk[:, par_g, c * Q:(c + 1) * Q], qT[:, par, c, s],
                                   start=False, stop=(c == 1), skip_group_check=True)
                mm.then_inc(sb_mm, 1)

            def weigh(g, par_g, b, tau, first_tile):
                pe.wait_ge(v_ev, 2 * g + 2)
                if b == 0 and not first_tile:
                    pe.wait_ge(on_ready, tau)
                pe.wait_ge(exp_done, 3 * g + 3)
                for t in range(KT):
                    for h in range(H):
                        c = h % 4
                        pe.matmul(oV[32 * c:32 * c + 32, b, h // 4, :], pT[:, par_g, t, h * Q:(h + 1) * Q],
                                  vS[:, par_g, t, h, :], start=(b == 0 and t == 0 and h < 4), stop=False,
                                  skip_group_check=True)
                s = slice(b * Q, (b + 1) * Q)
                for c in range(4):
                    mm = pe.matmul(oV[32 * c:32 * c + 32, b], pL[s, :],
                                   vblk[s].rearrange("p (g c) d -> p c g d", c=4)[:, c], start=False, stop=True,
                                   skip_group_check=True)
                mm.then_inc(pv_mm, 1)

            def transposes(src, n, m=P):
                for i in range(n):
                    mm = pe.transpose(psX[0:m, i * P:(i + 1) * P], src(i), ident[:])
                mm.then_inc(step_mm, 1)

            def p_step(tau, k, n):
                if k == 0:
                    pe.wait_ge(ln1, tau + 1)
                    if n is not None:
                        pe.wait_ge(step_ready, n)
                    transposes(lambda i: xn1[:, i * P:(i + 1) * P], 2)
                else:
                    pe.wait_ge(step_ready, n)
                    for m in range(2):
                        for c in range(2):
                            mm = pe.matmul(psX[:, m * P:(m + 1) * P], wq[:, c, m * P:(m + 1) * P], xT1[:, c, :],
                                           start=(c == 0), stop=(c == 1))
                    mm.then_inc(step_mm, 1)

            def epi(tau, e, n):
                if e in (0, 7):
                    wait_apart(pe, step_ready, n)
                else:
                    pe.wait_ge(step_ready, n)
                if e == 0:
                    wait_apart(pe, on_ready, tau + 1)
                    transposes(lambda b: on[:, b].rearrange("p g d -> p (g d)"), BT, 64)
                elif e == 1:
                    for c in range(4):
                        mm = pe.matmul(psX[:, 0:D], oT[:, c], wo[:, c, :], start=(c == 0), stop=(c == 3))
                    mm.then_inc(step_mm, 1)
                elif e == 2:
                    transposes(lambda i: xn2[:, i * P:(i + 1) * P], 2)
                elif e in (3, 4):
                    w = 2 * D if e == 3 else D
                    o = 0 if e == 3 else 2 * D
                    for c in range(2):
                        mm = pe.matmul(psX[:, 0:w], xT2[:, c, :], wqkv[:, c, o:o + w], start=(c == 0), stop=(c == 1))
                    mm.then_inc(step_mm, 1)
                elif e == 5:
                    transposes(lambda i: rot[:, i * P:(i + 1) * P], 4)
                elif e == 6:
                    pe.matmul(psX[:, :], ident_r[:], causal_r[:].unsqueeze(1).to_broadcast([P, H, Q]),
                              start=True, stop=False, skip_group_check=True)
                    for b in range(BT):
                        for c in range(2):
                            mm = pe.matmul(psX[b * Q:(b + 1) * Q, c * 256:(c + 1) * 256],
                                           qkT[:, 2 + c, b * Q:(b + 1) * Q], qblk2[:, c, b], start=False, stop=True,
                                           skip_group_check=True)
                    mm.then_inc(step_mm, 1)
                elif e == 7:
                    for h in range(H):
                        for b in range(BT):
                            s = slice(b * Q, (b + 1) * Q)
                            mm = pe.matmul(psX[s, h * (DH + 1):(h + 1) * (DH + 1)], pT2[s, h * Q:(h + 1) * Q],
                                           v2[s, h, :], start=(h == 0), stop=True,
                                           skip_group_check=True)
                    mm.then_inc(step_mm, 1)
                elif e == 8:
                    transposes(lambda i: o2[:, i * P:(i + 1) * P], 2)
                elif e == 9:
                    for c in range(2):
                        mm = pe.matmul(psX[:, 0:D], o2T[:, c, :], wout[:, c, :], start=(c == 0), stop=(c == 1))
                    mm.then_inc(step_mm, 1)

            def slot(tau, b, where, first, last):
                at = step_at(tau, b, where, first, last)
                if not at:
                    return
                s, n = at
                if isinstance(s, str):
                    p_step(tau + 1, int(s[1]), n)
                else:
                    epi(tau - lag(s), s, n)

            def body(tau, par, first, last):
                for b in range(BT):
                    g = 4 * tau + b
                    score_rows(g, b % 2, 0, first=first and b == 0)
                    slot(tau, b, 0, first, last)
                    if not (last and b == 3):
                        if b < 3:
                            keys(tau, par, b + 1)
                        else:
                            keys(tau + 1, 1 - par, 0)
                    score_rows(g, b % 2, 1)
                    slot(tau, b, 1, first, last)
                    if b > 0:
                        weigh(g - 1, (b - 1) % 2, b - 1, tau, first)
                    elif not first:
                        weigh(g - 1, 1, 3, tau - 1, False)
                    if b < 3:
                        values(tau, par, b + 1)
                    elif not last:
                        values(tau + 1, 1 - par, 0)
                    slot(tau, b, 2, first, last)
                    score_cols(g, b % 2, par, b, first=first and b == 0)
                    slot(tau, b, 3, first, last)

            p_step(0, 0, None)
            p_step(0, 1, 1)
            keys(0, 0, 0, first=True)
            values(0, 0, 0)
            over_tiles(pe, body)
            weigh(4 * LAST + 3, 1, 3, LAST, False)
            for e, tau, n in final_steps():
                epi(tau, e, n)




def experts(nc, X, ident, mhalf, xs, ys, WrT, W1T, W2T, tri_d, rev_d, tid_d, out):
    TILES = X.shape[1]
    NS = SLOT_TILES(TILES)
    FC = F // P
    GS = min(8, TILES // 2)

    with ExitStack() as ctx:
        def sb(name, shape, dt=F32):
            return ctx.enter_context(nc.sbuf_tensor(name, shape, dt))

        def pb(name, shape, dt=F32):
            return ctx.enter_context(nc.psum_tensor(name, shape, dt))

        def sem(name):
            return ctx.enter_context(nc.semaphore(name))

        XN = sb("XN", [P, TILES, D])
        w1 = sb("w1", [P, E, 2, 2 * F])
        w2 = sb("w2", [P, E, FC, D])
        wr = sb("wr", [P, 2, E])
        tri = sb("tri", [P, P])
        ones = sb("ones", [P, P])
        rev = sb("rev", [P, E])
        tid = sb("tid", [1, NS])
        st3 = sb("st3", [P, TILES, 6])
        mean3 = sb("mean3", [P, TILES])
        sq3 = sb("sq3", [P, TILES])
        half3 = sb("half3", [P, TILES])
        var3 = sb("var3", [P, TILES])
        ve3 = sb("ve3", [P, TILES])
        rstd3 = sb("rstd3", [P, TILES])
        xb = sb("xb", [P, 2, D])
        xbT = sb("xbT", [P, 2, 2, P])
        lg = sb("lg", [P, TILES, E])
        lm = sb("lm", [P, TILES, E])
        eq = sb("eq", [P, TILES, E])
        top = sb("top", [P, K, TILES])
        first = sb("first", [P, K, TILES])
        hot = sb("hot", [P, K, TILES, E])
        both = sb("both", [P, TILES, E])
        gap = sb("gap", [P, TILES])
        egap = sb("egap", [P, TILES])
        wgt = sb("wgt", [P, K, TILES])
        tot = sb("tot", [P, TILES, E])
        scan = sb("scan", [P, 2, TILES, E])
        cnt_i = sb("cnt_i", [P, E], I32)
        cnt_t = sb("cnt_t", [P, E], I32)
        nt = sb("nt", [P, E])
        escan = sb("escan", [P, 2, E])
        base = sb("base", [P, E])
        posE = sb("posE", [P, TILES, E])
        posf = sb("posf", [P, K, TILES])
        pos = sb("pos", [P, K, TILES], U32)
        past = sb("past", [1, NS, E])
        tef = sb("tef", [1, NS])
        te = sb("te", [1, NS], I32)
        xrow = sb("xrow", [P, 2, D])
        xsT = sb("xsT", [P, 2, 2, P])
        sg = sb("sg", [P, 2, F])
        am = sb("am", [P, 2, F])
        aT = sb("aT", [P, 2, FC, P])
        yrow = sb("yrow", [P, 2, D])

        picked = XN[:].rearrange("p i d -> p (i d)")[:, 0:GS * K * D].rearrange("p (s k d) -> p s k d", s=GS, k=K)

        psT = pb("psT", [P, 512])
        psL = pb("psL", [P, 512])
        psG = [pb(f"psG{i}", [P, 512]) for i in range(2)]
        psV = [pb(f"psV{i}", [P, 512]) for i in range(2)]
        psAT = pb("psAT", [P, 512])
        psY = pb("psY", [P, 512])

        r_in = sem("r_in")
        w_in = sem("w_in2")
        ones_set = sem("ones_set2")
        stats3 = sem("stats3")
        var3_ready = sem("var3_ready")
        rstd_ready = sem("rstd_ready")
        xb_ready = sem("xb_ready")
        xb_mm = sem("xb_mm")
        xbT_ready = sem("xbT_ready")
        lg_mm = sem("lg_mm")
        kept_xn = sem("kept_xn")
        gap_ready = sem("gap_ready")
        exp_ready = sem("exp_ready")
        both_ready = sem("both_ready")
        rank_mm = sem("rank_mm")
        pos_ready = sem("pos_ready")
        te_ready = sem("te_ready")
        scattered = sem("scattered")
        dve_chain = sem("dve_chain2")
        pool_chain = sem("pool_chain2")
        xrow_in = [sem("xrow_in0"), sem("xrow_in1")]
        tx_mm = sem("tx_mm")
        xT_ready = sem("xT_ready")
        h_mm = sem("h_mm")
        silu_done = sem("silu_done")
        act_ready = sem("act_ready")
        at_mm = sem("at_mm")
        aT_ready = sem("aT_ready")
        y_mm = sem("y_mm")
        y_ready = sem("y_ready")
        y_out = [sem("y_out0"), sem("y_out1")]
        picked_in = [sem(f"picked_in{s}") for s in range(GS)]
        summed = sem("summed")
        row_out = [sem(f"row_out{s}") for s in range(GS)]

        block = ctx.enter_context(nc.Block())

        @block.sync
        def _(sp):
            for dst, src in ((wr, WrT), (tri, tri_d), (rev, rev_d), (tid, tid_d)):
                sp.dma_start(dst[:], src).then_inc(r_in, 16)
            for e in range(E):
                sp.dma_start(w1[:, e], W1T[:, e]).then_inc(w_in, 16)
                sp.dma_start(w2[:, e], W2T[:, e]).then_inc(w_in, 16)
            sp.wait_ge(scattered, 16 * K * TILES)

            def load(t, par):
                sp.dma_start(xrow[:, par], xs[bass.ds(t * P, P), :]).then_inc(xrow_in[par], 16)

            def store(t, par):
                sp.wait_ge(y_ready, t + 1)
                sp.dma_start(ys[bass.ds(t * P, P), :], yrow[:, par]).then_inc(y_out[par], 16)

            load(0, 0)
            load(1, 1)
            sp.wait_ge(tx_mm, 1)
            load(2, 0)
            sp.wait_ge(tx_mm, 2)
            load(3, 1)
            store(0, 0)
            with sp.Fori(0, NS // 2 - 2) as j:
                for par in range(2):
                    sp.wait_ge(tx_mm, 2 * j + par + 3)
                    load(2 * j + par + 4, par)
                    store(2 * j + par + 1, 1 - par)
            for t in range(NS - 3, NS):
                store(t, t % 2)
            with sp.Fori(0, TILES // GS) as j:
                for s in range(GS):
                    sp.wait_ge(summed, GS * j + s + 1)
                    sp.dma_start(out[bass.ds((GS * j + s) * P, P), :], picked[:, s, 0, :]).then_inc(row_out[s], 16)
            for s in range(GS):
                sp.wait_ge(row_out[s], 16 * (TILES // GS))

        @block.gpsimd
        def _(pool):
            chain = Chain(pool, pool_chain)
            pool.wait_ge(var3_ready, 1)
            chain.done(pool.tensor_scalar(ve3[:], var3[:], EPS, None, ALU.add))
            pool.tensor_tensor(rstd3[:], ve3[:], mhalf[:].to_broadcast([P, TILES]), ALU.pow).then_inc(rstd_ready, 1)
            with pool.Fori(0, TILES // 2) as j:
                for par in range(2):
                    pool.wait_ge(xb_ready, 2 * j + par + 1)
                    pool.tensor_copy(XN[:, bass.ds(2 * j + par, 1), :].rearrange("p a d -> p (a d)"),
                                     xb[:, par]).then_inc(kept_xn, 1)
            pool.wait_ge(kept_xn, TILES)
            pool.wait_ge(pos_ready, 1)
            for i in range(TILES):
                for k in range(K):
                    pool.indirect_dma_start(xs, bass.IndirectOffsetOnAxis(ap=pos[:, k, i:i + 1], axis=0),
                                            XN[:, i, :], None).then_inc(scattered, 16)
            for par in range(2):
                pool.wait_ge(y_out[par], 16 * (NS // 2))
            for i in range(TILES):
                s = i % GS
                if i >= GS:
                    pool.wait_ge(row_out[s], 16 * (i // GS))
                for k in range(K):
                    pool.indirect_dma_start(picked[:, s, k, :], None, ys,
                                            bass.IndirectOffsetOnAxis(ap=pos[:, k, i:i + 1], axis=0)
                                            ).then_inc(picked_in[s], 16)

        @block.scalar
        def _(act):
            with act.Fori(0, TILES // 2) as j:
                for par in range(2):
                    act.wait_ge(xb_mm, 2 * j + par + 1)
                    act.activation(xbT[:, par], psT[:, 0:D].rearrange("p (c n) -> p c n", c=2),
                                   ACT.Identity).then_inc(xbT_ready, 1)
            act.wait_ge(gap_ready, 1)
            act.activation(egap[:], gap[:], ACT.Exp).then_inc(exp_ready, 1)

            def rows(t, par, head):
                act.wait_ge(tx_mm, t + 1)
                if not head:
                    act.wait_ge(h_mm, 2 * (t - 1))
                act.activation(xsT[:, par], psT[:, 0:D].rearrange("p (c n) -> p c n", c=2),
                               ACT.Identity).then_inc(xT_ready, 1)

            def silu(t, par, head):
                act.wait_ge(h_mm, 2 * t + 1)
                if not head:
                    act.wait_ge(act_ready, t - 1)
                act.activation(sg[:, par], psG[par][:, :], ACT.Silu).then_inc(silu_done, 1)

            def hidden(t, par, head):
                act.wait_ge(at_mm, t + 1)
                if not head:
                    act.wait_ge(y_mm, t - 1)
                act.activation(aT[:, par], psAT[:, :].rearrange("p (c n) -> p c n", c=FC),
                               ACT.Identity).then_inc(aT_ready, 1)

            def body(t, par, first, last):
                if not last:
                    rows(t + 1, 1 - par, first)
                if not first:
                    hidden(t - 1, 1 - par, False)
                silu(t, par, False)

            rows(0, 0, True)
            rows(1, 1, True)
            silu(0, 0, True)
            rows(2, 0, False)
            hidden(0, 0, True)
            silu(1, 1, True)
            rows(3, 1, False)
            hidden(1, 1, True)
            silu(2, 0, False)
            with act.Fori(0, (NS - 4) // 2) as j:
                body(2 * j + 3, 1, False, False)
                body(2 * j + 4, 0, False, False)
            body(NS - 1, 1, False, True)
            hidden(NS - 1, 1, False)

        @block.vector
        def _(dve):
            chain = Chain(dve, dve_chain)
            dve.memset(ones[:], 1.0).then_inc(ones_set, 1)
            with dve.Fori(0, TILES // 2) as j:
                for par in range(2):
                    i = 2 * j + par
                    xi = X[:, bass.ds(i, 1), :].rearrange("p a d -> p (a d)")
                    dve.bn_stats(st3[:, bass.ds(i, 1), :].rearrange("p a d -> p (a d)"), xi).then_inc(stats3, 1)
            dve.wait_ge(stats3, TILES)
            dve.tensor_tensor(mean3[:], st3[:, :, 1], st3[:, :, 4], ALU.add)
            dve.tensor_tensor(sq3[:], st3[:, :, 2], st3[:, :, 5], ALU.add)
            chain.done(dve.tensor_tensor(half3[:], st3[:, :, 1], st3[:, :, 4], ALU.subtract))
            dve.tensor_tensor(half3[:], half3[:], half3[:], ALU.mult)
            chain.done(dve.tensor_scalar(mean3[:], mean3[:], 0.5, None, ALU.mult))
            chain.done(dve.tensor_scalar(half3[:], half3[:], 0.25, None, ALU.mult))
            dve.scalar_tensor_tensor(var3[:], sq3[:], 1.0 / D, half3[:], ALU.mult, ALU.add).then_inc(var3_ready, 1)
            dve.wait_ge(rstd_ready, 1)

            def norm(i, par, head):
                if not head:
                    dve.wait_ge(xb_mm, i - 1)
                    dve.wait_ge(kept_xn, i - 1)
                dve.tensor_scalar(xb[:, par], X[:, bass.ds(i, 1), :].rearrange("p a d -> p (a d)"),
                                  mean3[:, bass.ds(i, 1)],
                                  rstd3[:, bass.ds(i, 1)], ALU.subtract, ALU.mult).then_inc(xb_ready, 1)

            norm(0, 0, True)
            norm(1, 1, True)
            with dve.Fori(0, TILES // 2 - 1) as j:
                norm(2 * j + 2, 0, False)
                norm(2 * j + 3, 1, False)
            dve.wait_ge(r_in, 16 * 4)

            dve.wait_ge(lg_mm, TILES)
            chain.done(dve.tensor_copy(lg[:], psL[:, 0:TILES * E].rearrange("p (i e) -> p i e", e=E)))
            rv = rev[:].unsqueeze(1).to_broadcast([P, TILES, E])
            cur = lg
            for k in range(K):
                chain.done(dve.reduce_max(top[:, k], cur[:], AX_X))
                chain.done(dve.tensor_tensor(eq[:], cur[:], top[:, k].unsqueeze(2).to_broadcast([P, TILES, E]),
                                             ALU.is_equal))
                chain.done(dve.tensor_tensor(eq[:], eq[:], rv, ALU.mult))
                chain.done(dve.reduce_max(first[:, k], eq[:], AX_X))
                chain.done(dve.tensor_tensor(hot[:, k], rv, first[:, k].unsqueeze(2).to_broadcast([P, TILES, E]),
                                             ALU.is_equal))
                if k == 0:
                    chain.done(dve.scalar_tensor_tensor(lm[:], hot[:, 0], -3e38, lg[:], ALU.mult, ALU.add))
                    cur = lm
            dve.tensor_tensor(gap[:], top[:, 1], top[:, 0], ALU.subtract).then_inc(gap_ready, 1)
            dve.tensor_tensor(both[:], hot[:, 0], hot[:, 1], ALU.add).then_inc(both_ready, 1)
            dve.wait_ge(exp_ready, 1)
            chain.done(dve.tensor_scalar(gap[:], egap[:], 1.0, None, ALU.add))
            chain.done(dve.reciprocal(wgt[:, 0], gap[:]))
            chain.done(dve.tensor_tensor(wgt[:, 1], egap[:], wgt[:, 0], ALU.mult))

            dve.wait_ge(rank_mm, 1)
            chain.done(dve.tensor_copy(tot[:], psG[0][:, TILES * E:2 * TILES * E].rearrange("p (i e) -> p i e", e=E)))
            chain.done(dve.tensor_copy(scan[:, 0], tot[:]))
            a, s = 0, 1
            while s < TILES:
                dve.tensor_copy(scan[:, 1 - a, 0:s], scan[:, a, 0:s])
                chain.done(dve.tensor_tensor(scan[:, 1 - a, s:TILES], scan[:, a, s:TILES],
                                             scan[:, a, 0:TILES - s], ALU.add))
                a, s = 1 - a, 2 * s
            chain.done(dve.tensor_scalar(cnt_i[:], scan[:, a, TILES - 1], float(P - 1), None, ALU.add))
            chain.done(dve.tensor_scalar(cnt_t[:], cnt_i[:], 7, None, ALU.logical_shift_right))
            chain.done(dve.tensor_copy(nt[:], cnt_t[:]))
            chain.done(dve.tensor_copy(escan[:, 0], nt[:]))
            b, s = 0, 1
            while s < E:
                dve.tensor_copy(escan[:, 1 - b, 0:s], escan[:, b, 0:s])
                chain.done(dve.tensor_tensor(escan[:, 1 - b, s:E], escan[:, b, s:E], escan[:, b, 0:E - s], ALU.add))
                b, s = 1 - b, 2 * s
            chain.done(dve.tensor_tensor(base[:], escan[:, b], nt[:], ALU.subtract))
            chain.done(dve.tensor_scalar(base[:], base[:], float(P), None, ALU.mult))
            chain.done(dve.tensor_tensor(posE[:], scan[:, a], tot[:], ALU.subtract))
            chain.done(dve.tensor_tensor(posE[:], posE[:],
                                         psG[0][:, 0:TILES * E].rearrange("p (i e) -> p i e", e=E), ALU.add))
            chain.done(dve.tensor_tensor(posE[:], posE[:], base[:].unsqueeze(1).to_broadcast([P, TILES, E]), ALU.add))
            for k in range(K):
                chain.done(dve.tensor_tensor(eq[:], hot[:, k], posE[:], ALU.mult))
                chain.done(dve.reduce_sum(posf[:, k], eq[:], AX_X))
            dve.tensor_copy(pos[:], posf[:]).then_inc(pos_ready, 1)
            chain.done(dve.tensor_tensor(past[:], tid[:].unsqueeze(2).to_broadcast([1, NS, E]),
                                         escan[0:1, b].unsqueeze(1).to_broadcast([1, NS, E]), ALU.is_ge))
            chain.done(dve.reduce_sum(tef[:], past[:], AX_X))
            dve.tensor_scalar(te[:], tef[:], float(E - 1), None, ALU.min).then_inc(te_ready, 1)

            def gate(t, par, head):
                dve.wait_ge(silu_done, t + 1)
                dve.wait_ge(h_mm, 2 * t + 2)
                if not head:
                    dve.wait_ge(at_mm, t - 1)
                dve.tensor_tensor(am[:, par], psV[par][:, :], sg[:, par], ALU.mult).then_inc(act_ready, 1)

            def result(t, par, j1, head):
                dve.wait_ge(y_mm, t + 1)
                if not head:
                    dve.wait_ge(y_out[par], j1)
                dve.tensor_copy(yrow[:, par], psY[:, 0:D]).then_inc(y_ready, 1)

            gate(0, 0, True)
            gate(1, 1, True)
            result(0, 0, 0, True)
            gate(2, 0, False)
            result(1, 1, 0, True)
            with dve.Fori(0, (NS - 4) // 2) as j:
                gate(2 * j + 3, 1, False)
                result(2 * j + 2, 0, 16 * (j + 1), False)
                gate(2 * j + 4, 0, False)
                result(2 * j + 3, 1, 16 * (j + 1), False)
            gate(NS - 1, 1, False)
            result(NS - 2, 0, 16 * (NS // 2 - 1), False)
            result(NS - 1, 1, 16 * (NS // 2 - 1), False)
            links = chain.n + chain.base
            with dve.Fori(0, TILES // GS) as j:
                chain.n, chain.base = 0, links + GS * j
                for s in range(GS):
                    i = GS * j + s
                    dve.wait_ge(picked_in[s], 16 * K * (j + 1))
                    acc = picked[:, s, 0, :]
                    xi = X[:, bass.ds(i, 1), :].rearrange("p a d -> p (a d)")
                    chain.done(dve.scalar_tensor_tensor(acc, acc, wgt[:, 0, bass.ds(i, 1)], xi, ALU.mult, ALU.add))
                    dve.scalar_tensor_tensor(acc, picked[:, s, 1, :], wgt[:, 1, bass.ds(i, 1)], acc, ALU.mult,
                                             ALU.add).then_inc(summed, 1)

        @block.tensor
        def _(pe):
            pe.wait_ge(r_in, 16 * 4)
            pe.wait_ge(ones_set, 1)

            def rowsT(i, par, head):
                pe.wait_ge(xb_ready, i + 1)
                if not head:
                    pe.wait_ge(xbT_ready, i)
                for c in range(2):
                    mm = pe.transpose(psT[:, c * P:(c + 1) * P], xb[:, par, c * P:(c + 1) * P], ident[:])
                mm.then_inc(xb_mm, 1)

            def logits(i, par):
                pe.wait_ge(xbT_ready, i + 1)
                for c in range(2):
                    mm = pe.matmul(psL[:, bass.ds(i * E, E)], xbT[:, par, c, :], wr[:, c, :], start=(c == 0),
                                   stop=(c == 1))
                mm.then_inc(lg_mm, 1)

            rowsT(0, 0, True)
            logits(0, 0)
            rowsT(1, 1, False)
            logits(1, 1)
            with pe.Fori(0, TILES // 2 - 1) as j:
                for par in range(2):
                    rowsT(2 * j + 2 + par, par, False)
                    logits(2 * j + 2 + par, par)
            pe.wait_ge(both_ready, 1)
            bv = both[:].rearrange("p i e -> p (i e)")
            pe.matmul(psG[0][:, 0:TILES * E], tri[:], bv, start=True, stop=True)
            pe.matmul(psG[0][:, TILES * E:2 * TILES * E], ones[:], bv, start=True, stop=True).then_inc(rank_mm, 1)
            pe.wait_ge(te_ready, 1)
            pe.wait_ge(w_in, 16 * 2 * E)

            def rows(t, par, j1, head):
                pe.wait_ge(xrow_in[par], j1)
                if not head:
                    pe.wait_ge(xT_ready, t)
                for c in range(2):
                    mm = pe.transpose(psT[:, c * P:(c + 1) * P], xrow[:, par, c * P:(c + 1) * P], ident[:])
                mm.then_inc(tx_mm, 1)

            def up(t, par, e, head):
                pe.wait_ge(xT_ready, t + 1)
                if not head:
                    pe.wait_ge(act_ready, t - 1)
                for bank, o in ((psG[par], F), (psV[par], 0)):
                    for c in range(2):
                        mm = pe.matmul(bank[:, :], xsT[:, par, c, :], w1[:, bass.ds(e, 1), c, o:o + F],
                                       start=(c == 0), stop=(c == 1))
                    mm.then_inc(h_mm, 1)

            def turn(t, par, head):
                pe.wait_ge(act_ready, t + 1)
                if not head:
                    pe.wait_ge(aT_ready, t)
                for c in range(FC):
                    mm = pe.transpose(psAT[:, c * P:(c + 1) * P], am[:, par, c * P:(c + 1) * P], ident[:])
                mm.then_inc(at_mm, 1)

            def down(t, par, e, head):
                pe.wait_ge(aT_ready, t + 1)
                if not head:
                    pe.wait_ge(y_ready, t)
                for c in range(FC):
                    mm = pe.matmul(psY[:, 0:D], aT[:, par, c, :], w2[:, bass.ds(e, 1), c, :],
                                   start=(c == 0), stop=(c == FC - 1))
                mm.then_inc(y_mm, 1)

            def expert(t):
                return pe.value_load(te[0:1, bass.ds(t, 1)], min_val=0, max_val=E - 1)

            rows(0, 0, 16, True)
            rows(1, 1, 16, False)
            up(0, 0, expert(0), True)
            rows(2, 0, 32, False)
            turn(0, 0, True)
            up(1, 1, expert(1), True)
            down(0, 0, expert(0), True)
            rows(3, 1, 32, False)
            turn(1, 1, False)
            up(2, 0, expert(2), False)
            down(1, 1, expert(1), False)
            with pe.Fori(0, (NS - 4) // 2) as j:
                for par in range(2):
                    t = 2 * j + 3 + par
                    rows(t + 1, par, 16 * (j + 3), False)
                    turn(t - 1, par, False)
                    up(t, 1 - par, expert(t), False)
                    down(t - 1, par, expert(t - 1), False)
            turn(NS - 2, 0, False)
            up(NS - 1, 1, expert(NS - 1), False)
            down(NS - 2, 0, expert(NS - 2), False)
            turn(NS - 1, 1, False)
            down(NS - 1, 1, expert(NS - 1), False)



def kernel(x, ctx_512, L0_xattn_Wq, L0_xattn_bq, L0_xattn_Wk, L0_xattn_bk, L0_xattn_Wv, L0_xattn_bv, L0_xattn_Wo,
           L0_xattn_bo, L0_attn_W_qkv, L0_attn_W_out, L0_attn_b_out, L0_ffn_Wr, L0_ffn_W1, L0_ffn_W2):
    import numpy as np
    import concourse.bacc as bacc
    from concourse.bass_utils import run_bass_kernel_spmd

    x = np.asarray(x)
    B = x.shape[0]
    tiles = B * Q // P

    def rows(w):
        return np.asarray(w).reshape(-1, P, w.shape[-1]).transpose(1, 0, 2)

    def spread(b):
        return np.broadcast_to(np.asarray(b), (P, D))

    pos = np.arange(P) % Q
    ang = pos[:, None].astype(np.float32) * (1.0 / 10000.0 ** (np.arange(DH // 2, dtype=np.float32) / (DH // 2)))
    ang = ang.astype(np.float32)
    cos, sin = np.cos(ang), np.sin(ang)
    arrays = {
        "x": x.reshape(tiles, P, D).transpose(1, 0, 2),
        "ctxT": np.asarray(ctx_512).transpose(2, 0, 1).reshape(CD, -1),
        "Wq": rows(L0_xattn_Wq),
        "bq": np.asarray(L0_xattn_bq).reshape(2, P).T,
        "Wk": np.asarray(L0_xattn_Wk),
        "bk": np.asarray(L0_xattn_bk).reshape(2, P).T,
        "Wv": np.asarray(L0_xattn_Wv),
        "bvT": np.asarray(L0_xattn_bv).reshape(4, 4, DH).transpose(0, 2, 1).reshape(4 * DH, 4),
        "WoR": np.asarray(L0_xattn_Wo).reshape(4, 4, DH, D).transpose(0, 2, 1, 3).reshape(4 * DH, 4, D),
        "bo": spread(L0_xattn_bo),
        "Wqkv": rows(L0_attn_W_qkv),
        "Wout": rows(L0_attn_W_out),
        "bout": spread(L0_attn_b_out),
        "ident": np.eye(P, dtype=np.float32),
        "hmask": (np.arange(P)[:, None] // DH == np.arange(HC)[None]).astype(np.float32),
        "cos": np.stack([cos, cos], -1).reshape(P, DH),
        "sin": np.stack([-sin, sin], -1).reshape(P, DH),
        "causal": np.where(np.arange(Q)[None] >= pos[:, None], 0, -1e9 * DH ** 0.5).astype(np.float32),
        "fold": -(np.arange(P)[:, None] % Q == np.arange(Q)[None]).astype(np.float32),
        "hsel": (np.arange(P)[:, None] % Q == np.arange(H)[None]).astype(np.float32),
        "chead": (np.arange(P)[:, None] // Q == np.arange(BT)[None]).astype(np.float32),
        "WrT": np.asarray(L0_ffn_Wr).T.reshape(2, P, E).transpose(1, 0, 2),
        "W1T": np.asarray(L0_ffn_W1).transpose(2, 0, 1).reshape(2, P, E, 2 * F).transpose(1, 2, 0, 3),
        "W2T": np.asarray(L0_ffn_W2).transpose(2, 0, 1).reshape(F // P, P, E, D).transpose(1, 2, 0, 3),
        "tri": np.triu(np.ones((P, P), np.float32), 1),
        "rev": np.broadcast_to(E - np.arange(E, dtype=np.float32), (P, E)),
        "tid": np.arange(SLOT_TILES(tiles), dtype=np.float32)[None],
    }
    arrays = {f"in_{k}": np.ascontiguousarray(v) for k, v in arrays.items()}
    nc = bacc.Bacc("TRN2", target_bir_lowering=False, num_devices=1)
    args = [nc.dram_tensor(k, v.shape, mybir.dt.from_np(v.dtype), kind="ExternalInput").ap()
            for k, v in arrays.items()]
    out = nc.dram_tensor("out", (tiles * P, D), F32, kind="ExternalOutput").ap()
    perceiver(nc, *args, out)
    r = run_bass_kernel_spmd(nc, [arrays], core_ids=[0])
    return r.results[0]["out"].reshape(B, Q, D)
```

```python
from contextlib import ExitStack

import concourse.bass as bass
from concourse import mybir

F32 = mybir.dt.float32
F32R = mybir.dt.float32r
I32 = mybir.dt.int32
U32 = mybir.dt.uint32
ALU = mybir.AluOpType
ACT = mybir.ActivationFunctionType
AX_X = mybir.AxisListType.X

P = 128
Q = 32
D = 256
CD = 128
KV = 257
H = 16
DH = D // H
BT = P // Q
HC = H // 2
KT = 2
EPS = 1e-5
E = 8
F = 512
K = 2
DVE_LINKS = 24
POOL_LINKS = 4


def SLOT_TILES(tiles):
    return K * tiles + E


class Chain:

    def __init__(self, eng, sem):
        self.eng, self.sem, self.base, self.n = eng, sem, 0, 0

    def done(self, ins, wait=None):
        self.n += 1
        ins.then_inc(self.sem, 1)
        if wait:
            wait(self.eng, self.sem, self.base + self.n)
        else:
            self.eng.wait_ge(self.sem, self.base + self.n)


def perceiver(nc, x, ctxT, Wq, bq, Wk, bk, Wv, bvT, WoR, bo, Wqkv, Wout, bout, ident_d, hmask_d, cos_d, sin_d,
              causal_d, fold_d, hsel_d, chead_d, WrT, W1T, W2T, tri_d, rev_d, count_d, id_d, out):
    TILES = x.shape[1]
    assert TILES % 2 == 0 and TILES >= 6

    xs = nc.dram_tensor("token_rows", (TILES * P, D), F32, kind="Internal").ap()
    ys = nc.dram_tensor("slot_outputs", (SLOT_TILES(TILES) * P, D), F32, kind="Internal").ap()

    with ExitStack() as whole:
        def kept(name, shape, dt=F32):
            return whole.enter_context(nc.sbuf_tensor(name, shape, dt))

        X = kept("X", [P, TILES, D])
        st3 = kept("st3", [P, TILES, 6])
        ident = kept("ident", [P, P])
        mhalf = kept("mhalf", [P, 1])
        attentions(nc, X, st3, ident, mhalf, x, ctxT, Wq, bq, Wk, bk, Wv, bvT, WoR, bo, Wqkv, Wout, bout, ident_d,
                   hmask_d, cos_d, sin_d, causal_d, fold_d, hsel_d, chead_d)
        experts(nc, X, st3, ident, mhalf, xs, ys, WrT, W1T, W2T, tri_d, rev_d, count_d, id_d, out)


def attentions(nc, X, st3, ident, mhalf, x, ctxT, Wq, bq, Wk, bk, Wv, bvT, WoR, bo, Wqkv, Wout, bout, ident_d,
               hmask_d, cos_d, sin_d, causal_d, fold_d, hsel_d, chead_d):
    TILES = X.shape[1]
    LAST = TILES - 1
    CW = BT * KV

    with ExitStack() as ctx:
        def sb(name, shape, dt=F32):
            return ctx.enter_context(nc.sbuf_tensor(name, shape, dt))

        def pb(name, shape, dt=F32):
            return ctx.enter_context(nc.psum_tensor(name, shape, dt))

        def sem(name):
            return ctx.enter_context(nc.semaphore(name))

        cT = sb("cT", [P, 2, CW])
        wq = sb("wq", [P, 2, D])
        wk = sb("wk", [P, D])
        wv = sb("wv", [P, D])
        wo = sb("wo", [64, 4, D])
        wqkv = sb("wqkv", [P, 2, 3 * D])
        wout = sb("wout", [P, 2, D])
        bq_s = sb("bq_s", [P, 2])
        bk_s = sb("bk_s", [P, 2])
        bv_s = sb("bv_s", [64, 4])
        bo_s = sb("bo_s", [P, D])
        bout_s = sb("bout_s", [P, D])
        hmask = sb("hmask", [P, HC])
        cos_s = sb("cos_s", [P, DH])
        sin_s = sb("sin_s", [P, DH])
        causal = sb("causal", [P, Q])
        causal_r = sb("causal_r", [P, Q], F32R)
        ident_r = sb("ident_r", [P, P], F32R)
        neg1 = sb("neg1", [P, P], F32R)
        stat = sb("stat", [P, 2, 6])
        mv = sb("mv", [P, 2, 2])
        rstd = sb("rstd", [P, 2])
        vareps = sb("vareps", [P, 2])
        xn1 = sb("xn1", [P, D])
        xT1 = sb("xT1", [P, 2, P])
        qT = sb("qT", [P, 2, 2, P])
        qblk = sb("qblk", [P, 2, 2, HC, Q])
        qblk_r = sb("qblk_r", [P, 2, 2, HC, Q], F32R)
        kT = sb("kT", [P, 2, 2, KV])
        kT_r = sb("kT_r", [P, 2, 2, KV + 1], F32R)
        vS = sb("vS", [P, 2, KT, H, DH + 1])
        kblk = sb("kblk", [P, 2, 2 * (Q + HC)])
        vblk = sb("vblk", [P, H, DH + 1])
        mblk = sb("mblk", [P, 2, Q], F32R)
        pL = sb("pL", [P, Q])
        fold = sb("fold", [P, Q])
        hsel = sb("hsel", [P, H])
        chead = sb("chead", [P, BT])
        mx = sb("mx", [P, 2, 4])
        mdiag = sb("mdiag", [P, 2, 4, P], F32R)
        pT = sb("pT", [P, 2, KT, H * Q])
        rs = sb("rs", [P, BT, 4])
        on = sb("on", [P, BT, 4, DH])
        oT = sb("oT", [64, 4, BT, Q])
        tmp = sb("tmp", [P, D])
        xn2 = sb("xn2", [P, D])
        xT2 = sb("xT2", [P, 2, P])
        rot = sb("rot", [P, 2 * D])
        swp = sb("swp", [P, 2 * D])
        v2 = sb("v2", [P, H, DH + 1])
        qkT = sb("qkT", [P, 4, P])
        qblk2 = sb("qblk2", [P, 2, BT, HC, Q])
        s2 = sb("s2", [P, H, Q])
        m2 = sb("m2", [P, H])
        r2 = sb("r2", [P, H])
        pT2 = sb("pT2", [P, H * Q])
        o2 = sb("o2", [P, D])
        o2T = sb("o2T", [P, 2, P])

        psP = [pb(f"psP{i}", [P, 512]) for i in range(2)]
        psA = [pb(f"psA{i}", [P, 512]) for i in range(2)]
        psB = [pb(f"psB{i}", [P, 512]) for i in range(2)]
        psO = pb("psO", [P, 512])
        psX = pb("psX", [P, 512])
        oV = psO[:, 0:BT * 4 * (DH + 1)].rearrange("p (b g d) -> p b g d", b=BT, g=4)

        x_in = [sem("x_in0"), sem("x_in1")]
        w_in = sem("w_in")
        w2_in = sem("w2_in")
        ctx_in = [sem("ctx_in0"), sem("ctx_in1")]
        ones_set = sem("ones_set")
        mask_ready = sem("mask_ready")
        k_mm = sem("k_mm")
        k_ev = sem("k_ev")
        kr_ready = sem("kr_ready")
        kblk_ready = sem("kblk_ready")
        qr_ready = sem("qr_ready")
        v_mm = sem("v_mm")
        v_ev = sem("v_ev")
        a_mm = sem("a_mm")
        max_done = sem("max_done")
        d_ready = sem("d_ready")
        sb_mm = sem("sb_mm")
        exp_done = sem("exp_done")
        pv_mm = sem("pv_mm")
        on_ready = sem("on_ready")
        q_ready = sem("q_ready")
        qblk_ready = sem("qblk_ready")
        var1 = sem("var1")
        var2 = sem("var2")
        rstd1 = sem("rstd1")
        rstd2 = sem("rstd2")
        ln1 = sem("ln1")
        step_mm = sem("step_mm")
        step_ready = sem("step_ready")
        tr_copied = sem("tr_copied")
        q2_ready = sem("q2_ready")
        sub_done = sem("sub_done")
        exp2_done = sem("exp2_done")
        dve_chain = sem("dve_chain")
        pool_chain = sem("pool_chain")
        carried = sem("carried")
        N_W = 11
        N_W2 = 8
        N_SET = 6

        def wait_apart(eng, semaphore, value):
            eng.wait_ge(semaphore, value)
            if not isinstance(value, int):
                eng.sem_inc(carried, 1)

        STEPS = ((8, "P0", "P1", 0), (9, 1, None, 2), (None, 3, 4, 5), (None, 6, None, 7))
        LATE = (8, 9)
        E9_AT = next((b, i) for b, row in enumerate(STEPS) for i, s in enumerate(row) if s == 9)
        ORDER = [s for row in STEPS for s in row if s is not None]
        BEFORE = 4 + len(ORDER) - len(LATE)

        def lag(s):
            return 2 if s in LATE else 1

        def steps_of(tau, first, last):
            if first:
                return ["P0", "P1"]
            return [s for s in ORDER if not (last and isinstance(s, str)) and not (
                isinstance(tau, int) and tau == 1 and s in LATE)]

        def step_at(tau, b, where, first, last):
            s = STEPS[b][where]
            mine = steps_of(tau, first, last)
            if s is None or s not in mine:
                return None
            if first:
                return s, 2 + mine.index(s)
            if isinstance(tau, int) and tau == 1:
                return s, 4 + mine.index(s)
            return s, BEFORE + (tau - 2) * len(ORDER) + mine.index(s)

        def final_steps():
            n = BEFORE + (LAST - 2) * len(ORDER) + len(steps_of(LAST, False, True))
            rest = [(e, LAST - 1) for e in LATE] + [(e, LAST) for e in range(10)]
            return [(e, tau, n + i) for i, (e, tau) in enumerate(rest)]

        def spread_chunk(eng, c):
            src = qkT[:, c, :].rearrange("p (b q) -> p b q", b=BT)
            return eng.tensor_tensor(qblk2[:, c], src.unsqueeze(2).to_broadcast([P, BT, HC, Q]),
                                     hmask[:].unsqueeze(1).unsqueeze(3).to_broadcast([P, BT, HC, Q]), ALU.mult)

        def ctx_wait(eng, tau, par):
            eng.wait_ge(ctx_in[par], (tau - par) * 8 + 16)

        def over_tiles(eng, body, chain=None, links=0):
            body(0, 0, True, False)
            eng.wait_ge(w2_in, 16 * N_W2)
            eng.wait_ge(x_in[1], 16)
            body(1, 1, False, False)
            start = chain.n if chain else 0
            with eng.Fori(0, (TILES - 4) // 2) as j:
                if chain:
                    chain.base = j * links
                body(2 * j + 2, 0, False, False)
                body(2 * j + 3, 1, False, False)
            if chain:
                assert chain.n - start == links, chain.n - start
                chain.base = ((TILES - 4) // 2 - 1) * links
            body(LAST - 1, 0, False, False)
            body(LAST, 1, False, True)

        block = ctx.enter_context(nc.Block())

        @block.sync
        def _(sp):
            sp.dma_start(X[:, 0:3, :], x[:, 0:3, :]).then_inc(x_in[0], 16)
            for dst, src in ((ident, ident_d), (wq, Wq), (bq_s, bq), (hmask, hmask_d), (wk, Wk), (wv, Wv),
                             (bk_s, bk), (fold, fold_d), (hsel, hsel_d), (chead, chead_d), (causal, causal_d)):
                sp.dma_start(dst[:], src).then_inc(w_in, 16)

            def load_ctx(tau, par):
                sp.dma_start(cT[:, par, :], ctxT[:, bass.ds(tau * CW, CW)]).then_inc(ctx_in[par], 16)

            load_ctx(0, 0)
            load_ctx(1, 1)
            for dst, src in ((wo, WoR), (bv_s, bvT), (bo_s, bo), (wqkv, Wqkv), (cos_s, cos_d), (sin_s, sin_d),
                             (wout, Wout), (bout_s, bout)):
                sp.dma_start(dst[:], src).then_inc(w2_in, 16)
            sp.dma_start(X[:, 3:TILES, :], x[:, 3:TILES, :]).then_inc(x_in[1], 16)
            with sp.Fori(0, (TILES - 2) // 2) as j:
                sp.wait_ge(v_mm, 16 * j + 8)
                load_ctx(2 * j + 2, 0)
                sp.wait_ge(v_mm, 16 * j + 16)
                load_ctx(2 * j + 3, 1)

        @block.gpsimd
        def _(pool):
            chain = Chain(pool, pool_chain)
            chain.done(pool.memset(mhalf[:], -0.5))
            pool.wait_ge(w_in, 16 * N_W)

            def inv_std(k, tau, var, done):
                wait_apart(pool, var, tau + 1)
                chain.done(pool.tensor_scalar(vareps[:, k:k + 1], mv[:, k, 1:2], EPS, None, ALU.add))
                pool.tensor_tensor(rstd[:, k:k + 1], vareps[:, k:k + 1], mhalf[:], ALU.pow).then_inc(done, 1)

            def spread_q(tau, par, b):
                g = 4 * tau + b
                pool.wait_ge(q_ready, tau + 1)
                if not (isinstance(tau, int) and g < 2):
                    pool.wait_ge(sb_mm, 3 * (g - 1))
                src = qT[:, par, :, b * Q:(b + 1) * Q]
                pool.tensor_tensor(qblk[:, b % 2], src.unsqueeze(2).to_broadcast([P, 2, HC, Q]),
                                   hmask[:].unsqueeze(1).unsqueeze(3).to_broadcast([P, 2, HC, Q]),
                                   ALU.mult).then_inc(qblk_ready, 1)

            def spread_k(g, par_g):
                pool.wait_ge(k_ev, 2 * g + 2)
                dst = kblk[:, par_g].rearrange("p (c w) -> p c w", c=2)[:, :, 0:HC]
                pool.tensor_tensor(dst, kT[:, par_g, :, KV - 1:KV].to_broadcast([P, 2, HC]),
                                   hmask[:].unsqueeze(1).to_broadcast([P, 2, HC]), ALU.mult).then_inc(kblk_ready, 1)

            def spread_q2(n):
                pool.wait_ge(tr_copied, n)
                spread_chunk(pool, 0).then_inc(step_ready, 1)

            def body(tau, par, first, last):
                for b in range(BT):
                    if b < 3:
                        spread_q(tau, par, b + 1)
                        spread_k(4 * tau + b + 1, (b + 1) % 2)
                    elif not last:
                        spread_q(tau + 1, 1 - par, 0)
                        spread_k(4 * tau + 4, 0)
                    if b == 2 and not (isinstance(tau, int) and tau + 2 > LAST):
                        inv_std(0, tau + 2, var1, rstd1)
                    if b == 2 and not first:
                        spread_q2(tau)
                    if b == 0 and not first:
                        inv_std(1, tau - 1, var2, rstd2)

            inv_std(0, 0, var1, rstd1)
            inv_std(0, 1, var1, rstd1)
            pool.wait_ge(ones_set, N_SET)
            spread_q(0, 0, 0)
            spread_k(0, 0)
            over_tiles(pool, body, chain, POOL_LINKS)
            inv_std(1, LAST, var2, rstd2)
            spread_q2(LAST + 1)

        @block.scalar
        def _(act):
            act.wait_ge(w_in, 16 * N_W)

            def step_copy(dst, src, n, sem2=None):
                act.wait_ge(step_mm, n + 1)
                ins = act.activation(dst, src, ACT.Identity)
                ins.then_inc(sem2 or step_ready, 1)

            def x2v(t):
                return psX[:, 0:2 * P].rearrange("p (c n) -> p c n", c=2)

            def keys(g, par_g, first=False):
                for c in range(2):
                    act.wait_ge(k_mm, 2 * g + c + 1)
                    if not first:
                        act.wait_ge(sb_mm, 3 * (g - 1))
                    act.activation(kT[:, par_g, c, :], psP[c][:, 0:KV], ACT.Identity,
                                   bias=bk_s[:, c:c + 1]).then_inc(k_ev, 1)
                act.wait_ge(k_ev, 2 * g + 2)
                if not first:
                    act.wait_ge(a_mm, 4 * (g - 1))
                act.activation(kT_r[:, par_g, :, 0:KV], kT[:, par_g], ACT.Identity).then_inc(kr_ready, 1)

            def exps(g, par_g, b, first=False):
                for t in range(KT):
                    act.wait_ge(sb_mm, 3 * g + t + 1)
                    if not first:
                        act.wait_ge(pv_mm, g - 1)
                    act.activation(pT[:, par_g, t, :], psB[(3 * par_g + t) % 2][:, :], ACT.Exp).then_inc(exp_done, 1)
                act.wait_ge(sb_mm, 3 * g + 3)
                s = slice(b * Q, (b + 1) * Q)
                act.activation(pL[s, :], psB[par_g % 2][s, 0:Q], ACT.Exp).then_inc(exp_done, 1)

            def slot(tau, b, where, first, last):
                at = step_at(tau, b, where, first, last)
                if not at:
                    return
                s, n = at
                if s == "P0":
                    step_copy(xT1[:], x2v(0), n)
                elif s != "P1":
                    epi(tau - lag(s), s, n)

            def epi(tau, e, n):
                if e == 2:
                    step_copy(xT2[:], x2v(0), n)
                elif e == 4:
                    step_copy(v2[:, :, 0:DH], psX[:, 0:D].rearrange("p (h d) -> p h d", h=H), n)
                elif e == 5:
                    step_copy(qkT[:], psX[:, :].rearrange("p (c n) -> p c n", c=4), n, tr_copied)
                elif e == 6:
                    act.wait_ge(sub_done, tau + 1)
                    act.activation(s2[:], s2[:], ACT.Exp, scale=DH ** -0.5).then_inc(exp2_done, 1)
                elif e == 8:
                    step_copy(o2T[:], x2v(0), n)

            def body(tau, par, first, last):
                for b in range(BT):
                    g = 4 * tau + b
                    slot(tau, b, 0, first, last)
                    if not (last and b == 3):
                        keys(g + 1, (b + 1) % 2, first=first and b == 0)
                    slot(tau, b, 1, first, last)
                    slot(tau, b, 2, first, last)
                    exps(g, b % 2, b, first=first and b < 2)
                    slot(tau, b, 3, first, last)

            step_copy(xT1[:], x2v(0), 0)
            keys(0, 0, first=True)
            over_tiles(act, body)
            for e, tau, n in final_steps():
                epi(tau, e, n)

        @block.vector
        def _(dve):
            chain = Chain(dve, dve_chain)
            dve.memset(neg1[:].bitcast(F32), -1.0).then_inc(ones_set, 1)
            dve.memset(kT_r[:].bitcast(F32)[:, :, :, KV:KV + 1], 0.0).then_inc(ones_set, 1)
            dve.memset(vS[:, :, :, :, DH:DH + 1], 1.0).then_inc(ones_set, 1)
            dve.memset(v2[:, :, DH:DH + 1], 1.0).then_inc(ones_set, 1)
            dve.memset(kblk[:], 0.0).then_inc(ones_set, 1)
            dve.memset(mblk[:].bitcast(F32), 0.0).then_inc(ones_set, 1)
            dve.wait_ge(x_in[0], 16)

            def norm(k, tau, src, dst, var, rdy, done):
                chain.done(dve.bn_stats(stat[:, k], src), wait_apart)
                dve.bn_aggr(mv[:, k], stat[:, k]).then_inc(var, 1)
                dve.wait_ge(var, tau + 1)
                dve.wait_ge(rdy, tau + 1)
                dve.tensor_scalar(dst, src, mv[:, k, 0:1], rstd[:, k:k + 1], ALU.subtract, ALU.mult).then_inc(done, 1)

            def xi(tau):
                return X[:, bass.ds(tau, 1), :].rearrange("p a d -> p (a d)")

            def query(tau, par, n, first):
                dve.wait_ge(step_mm, n + 1)
                if not first:
                    dve.wait_ge(qblk_ready, 4 * (tau - 1))
                    dve.wait_ge(sb_mm, 12 * (tau - 1))
                chain.done(dve.tensor_tensor(qT[:, par], psX[:, 0:2 * P].rearrange("p (c n) -> p c n", c=2),
                                             bq_s[:].unsqueeze(2).to_broadcast([P, 2, P]), ALU.add))
                chain.done(dve.tensor_scalar(qT[:, par], qT[:, par], DH ** -0.5, None, ALU.mult))
                dve.sem_inc(q_ready, 1)
                dve.sem_inc(step_ready, 1)

            def values(g, par_g, b, first=False):
                dve.wait_ge(v_mm, 2 * g + 1)
                if not first:
                    dve.wait_ge(pv_mm, g - 1)
                dve.tensor_copy(vS[:, par_g, 0:2, :, 0:DH],
                                psP[0][:, :].rearrange("p (t h d) -> p t h d", t=2, h=H)).then_inc(v_ev, 1)
                dve.wait_ge(v_mm, 2 * g + 2)
                s = slice(b * Q, (b + 1) * Q)
                dve.tensor_tensor(vblk[s, :, 0:DH], psP[1][s, 0:D].rearrange("p (h d) -> p h d", h=H),
                                  hsel[s, :].unsqueeze(2).to_broadcast([Q, H, DH]), ALU.mult).then_inc(v_ev, 1)

            def round_q(g, par_g):
                dve.wait_ge(qblk_ready, g + 1)
                dve.tensor_copy(qblk_r[:, par_g], qblk[:, par_g]).then_inc(qr_ready, 1)

            def maxima(g, par_g, half, first=False):
                for a in (2 * half, 2 * half + 1):
                    dve.wait_ge(a_mm, 4 * g + a + 1)
                    dve.reduce_max(mx[:, par_g, a:a + 1], psA[a % 2][:, 0:KV], AX_X).then_inc(max_done, 1)
                if half == 0:
                    return
                dve.wait_ge(max_done, 4 * g + 4)
                if not first:
                    dve.wait_ge(sb_mm, 3 * (g - 1))
                dve.tensor_tensor(mdiag[:, par_g], ident[:].unsqueeze(1).to_broadcast([P, 4, P]),
                                  mx[:, par_g].unsqueeze(2).to_broadcast([P, 4, P]),
                                  ALU.mult).then_inc(d_ready, 1)
                dve.tensor_tensor(mblk[:, par_g, 0:H].rearrange("p (g c) -> p g c", c=BT),
                                  chead[:].unsqueeze(1).to_broadcast([P, 4, BT]),
                                  mx[:, par_g].unsqueeze(2).to_broadcast([P, 4, BT]), ALU.mult).then_inc(d_ready, 1)

            def norm_o(tau):
                dve.wait_ge(pv_mm, 4 * tau + 4)
                chain.done(dve.reciprocal(rs[:], oV[:, :, :, DH]))
                dve.tensor_tensor(on[:], oV[:, :, :, 0:DH], rs[:].unsqueeze(3).to_broadcast([P, BT, 4, DH]),
                                  ALU.mult).then_inc(on_ready, 1)

            def epi(tau, e, n):
                if e == 0:
                    dve.wait_ge(step_mm, n + 1)
                    dve.tensor_tensor(oT[:].rearrange("p c b q -> p b c q"),
                                      psX[0:64, :].rearrange("p (b c q) -> p b c q", b=BT, c=4),
                                      bv_s[:].unsqueeze(1).unsqueeze(3).to_broadcast([64, BT, 4, Q]),
                                      ALU.add).then_inc(step_ready, 1)
                elif e == 1:
                    dve.wait_ge(step_mm, n + 1)
                    chain.done(dve.tensor_tensor(tmp[:], psX[:, 0:D], bo_s[:], ALU.add))
                    chain.done(dve.tensor_tensor(xi(tau), xi(tau), tmp[:], ALU.add), wait_apart)
                    norm(1, tau, xi(tau), xn2[:], var2, rstd2, step_ready)
                elif e == 3:
                    dve.wait_ge(step_mm, n + 1)
                    ps = psX[:, :].rearrange("p (h f e) -> p h f e", f=DH // 2, e=2)
                    sv = swp[:].rearrange("p (h f e) -> p h f e", f=DH // 2, e=2)
                    sn = sin_s[:].rearrange("p (f e) -> p f e", e=2)
                    for e2 in range(2):
                        dve.tensor_tensor(sv[:, :, :, e2], ps[:, :, :, 1 - e2],
                                          sn[:, :, e2].unsqueeze(1).to_broadcast([P, 2 * H, DH // 2]), ALU.mult)
                    chain.done(dve.tensor_tensor(rot[:].rearrange("p (h d) -> p h d", d=DH),
                                                 psX[:, :].rearrange("p (h d) -> p h d", d=DH),
                                                 cos_s[:].unsqueeze(1).to_broadcast([P, 2 * H, DH]), ALU.mult))
                    dve.tensor_tensor(rot[:], rot[:], swp[:], ALU.add).then_inc(step_ready, 1)
                elif e == 6:
                    dve.wait_ge(step_mm, n + 1)
                    chain.done(dve.transpose(s2[:].rearrange("p h k -> p (h k)"), psX[:, :]))
                    chain.done(dve.reduce_max(m2[:], s2[:], AX_X))
                    dve.tensor_tensor(s2[:], s2[:], m2[:].unsqueeze(2).to_broadcast([P, H, Q]),
                                      ALU.subtract).then_inc(sub_done, 1)
                    dve.wait_ge(exp2_done, tau + 1)
                    dve.transpose(pT2[:], s2[:].rearrange("p h k -> p (h k)")).then_inc(step_ready, 1)
                elif e == 7:
                    dve.wait_ge(step_mm, n + 1)
                    ov = psX[:, 0:H * (DH + 1)].rearrange("p (h d) -> p h d", h=H)
                    chain.done(dve.reciprocal(r2[:], ov[:, :, DH]))
                    dve.tensor_tensor(o2[:].rearrange("p (h d) -> p h d", h=H), ov[:, :, 0:DH],
                                      r2[:].unsqueeze(2).to_broadcast([P, H, DH]), ALU.mult).then_inc(step_ready, 1)
                elif e == 9:
                    dve.wait_ge(step_mm, n + 1)
                    chain.done(dve.tensor_tensor(tmp[:], psX[:, 0:D], bout_s[:], ALU.add))
                    dve.tensor_tensor(xi(tau), xi(tau), tmp[:], ALU.add).then_inc(step_ready, 1)

            def stats3(tau, n):
                wait_apart(dve, step_ready, n + 1)
                dve.bn_stats(st3[:, bass.ds(tau, 1), :].rearrange("p a d -> p (a d)"), xi(tau))

            def spread_q2(n):
                dve.wait_ge(tr_copied, n)
                spread_chunk(dve, 1).then_inc(q2_ready, 1)

            def slot(tau, par, b, where, first, last):
                at = step_at(tau, b, where, first, last)
                if not at:
                    return
                s, n = at
                if s == "P1":
                    query(tau + 1, 1 - par, n, first)
                elif s != "P0":
                    epi(tau - lag(s), s, n)

            def body(tau, par, first, last):
                for b in range(BT):
                    g = 4 * tau + b
                    maxima(g, b % 2, 0)
                    if b == 3 and not first:
                        spread_q2(tau)
                    slot(tau, par, b, 0, first, last)
                    maxima(g, b % 2, 1, first=first and b < 2)
                    if b == 0 and not first:
                        norm_o(tau - 1)
                    slot(tau, par, b, 1, first, last)
                    if not (last and b == 3):
                        values(g + 1, (b + 1) % 2, (b + 1) % BT, first=first and b == 0)
                    slot(tau, par, b, 2, first, last)
                    if not (last and b == 3):
                        round_q(g + 1, (b + 1) % 2)
                    if b == 2 and not (isinstance(tau, int) and tau + 2 > LAST):
                        norm(0, tau + 2, xi(tau + 2), xn1[:], var1, rstd1, ln1)
                    slot(tau, par, b, 3, first, last)
                if not first and not (isinstance(tau, int) and tau == 1):
                    at = step_at(tau, *E9_AT, first, last)
                    stats3(tau - 2, at[1])

            norm(0, 0, X[:, 0, :], xn1[:], var1, rstd1, ln1)
            dve.wait_ge(w_in, 16 * N_W)
            dve.tensor_copy(causal_r[:], causal[:]).then_inc(mask_ready, 1)
            dve.tensor_copy(ident_r[:], ident[:]).then_inc(mask_ready, 1)
            dve.tensor_copy(vblk[:, :, DH], hsel[:]).then_inc(mask_ready, 1)
            query(0, 0, 1, True)
            norm(0, 1, X[:, 1, :], xn1[:], var1, rstd1, ln1)
            values(0, 0, 0, first=True)
            round_q(0, 0)
            over_tiles(dve, body, chain, DVE_LINKS)
            norm_o(LAST)
            for e, tau, n in final_steps():
                epi(tau, e, n)
                if e == 5:
                    spread_q2(LAST + 1)
                if e == 9:
                    stats3(tau, n)

        @block.tensor
        def _(pe):
            pe.wait_ge(ones_set, N_SET)
            pe.wait_ge(mask_ready, 3)
            pe.wait_ge(w_in, 16 * N_W)

            def keys(tau, par, b, first=False):
                g = 4 * tau + b
                if b == 0:
                    ctx_wait(pe, tau, par)
                for c in range(2):
                    if not first:
                        pe.wait_ge(v_ev, 2 * g - 1 + c)
                    pe.matmul(psP[c][:, 0:KV], wk[:, c * P:(c + 1) * P], cT[:, par, b * KV:(b + 1) * KV],
                              start=True, stop=True).then_inc(k_mm, 1)

            def values(tau, par, b):
                g = 4 * tau + b
                pe.wait_ge(k_ev, 2 * g + 1)
                for t in range(2):
                    mm = pe.matmul(psP[0][:, t * D:(t + 1) * D], cT[:, par, b * KV + t * P:b * KV + (t + 1) * P],
                                   wv[:], start=True, stop=True)
                mm.then_inc(v_mm, 1)
                pe.wait_ge(k_ev, 2 * g + 2)
                pe.matmul(psP[1][b * Q:(b + 1) * Q, 0:D], cT[:, par, (b + 1) * KV - 1:(b + 1) * KV].to_broadcast([P, Q]),
                          wv[:], start=True, stop=True).then_inc(v_mm, 1)

            def score_rows(g, par_g, half, first=False):
                if half == 0:
                    pe.wait_ge(qr_ready, g + 1)
                    pe.wait_ge(kr_ready, g + 1)
                for a in (2 * half, 2 * half + 1):
                    if not (first and a < 2):
                        pe.wait_ge(max_done, 4 * g + a - 1)
                    pe.matmul(psA[a % 2][:, 0:KV + 1], qblk_r[:, par_g, a // 2, 4 * (a % 2):4 * (a % 2) + 4, :],
                              kT_r[:, par_g, a // 2, :], start=True, stop=True).then_inc(a_mm, 1)

            def score_cols(g, par_g, par, b, first=False):
                pe.wait_ge(d_ready, 2 * g + 1)
                pe.wait_ge(k_ev, 2 * g + 2)
                for t in range(KT):
                    bank = psB[(3 * par_g + t) % 2]
                    if not (first and t < 2):
                        pe.wait_ge(exp_done, 3 * g + t - 1)
                    pe.matmul(bank[:, :], neg1[:], mdiag[:, par_g], start=True, stop=False, skip_group_check=True)
                    for c in range(2):
                        mm = pe.matmul(bank[:, c * 256:(c + 1) * 256], kT[:, par_g, c, t * P:(t + 1) * P],
                                       qblk[:, par_g, c], start=False, stop=True, skip_group_check=True)
                    mm.then_inc(sb_mm, 1)
                wait_apart(pe, d_ready, 2 * g + 2)
                wait_apart(pe, kblk_ready, g + 1)
                wait_apart(pe, exp_done, 3 * g + 1)
                s = slice(b * Q, (b + 1) * Q)
                row = psB[par_g % 2][s, 0:Q]
                pe.matmul(row, mblk[:, par_g].bitcast(F32), fold[:], start=True, stop=False, skip_group_check=True)
                for c in range(2):
                    mm = pe.matmul(row, kblk[:, par_g, c * Q:(c + 1) * Q], qT[:, par, c, s],
                                   start=False, stop=(c == 1), skip_group_check=True)
                mm.then_inc(sb_mm, 1)

            def weigh(g, par_g, b, tau, first_tile):
                pe.wait_ge(v_ev, 2 * g + 2)
                if b == 0 and not first_tile:
                    pe.wait_ge(on_ready, tau)
                pe.wait_ge(exp_done, 3 * g + 3)
                for t in range(KT):
                    for h in range(H):
                        c = h % 4
                        pe.matmul(oV[32 * c:32 * c + 32, b, h // 4, :], pT[:, par_g, t, h * Q:(h + 1) * Q],
                                  vS[:, par_g, t, h, :], start=(b == 0 and t == 0 and h < 4), stop=False,
                                  skip_group_check=True)
                s = slice(b * Q, (b + 1) * Q)
                for c in range(4):
                    mm = pe.matmul(oV[32 * c:32 * c + 32, b], pL[s, :],
                                   vblk[s].rearrange("p (g c) d -> p c g d", c=4)[:, c], start=False, stop=True,
                                   skip_group_check=True)
                mm.then_inc(pv_mm, 1)

            def transposes(src, n, m=P):
                for i in range(n):
                    mm = pe.transpose(psX[0:m, i * P:(i + 1) * P], src(i), ident[:])
                mm.then_inc(step_mm, 1)

            def p_step(tau, k, n):
                if k == 0:
                    pe.wait_ge(ln1, tau + 1)
                    if n is not None:
                        pe.wait_ge(step_ready, n)
                    transposes(lambda i: xn1[:, i * P:(i + 1) * P], 2)
                else:
                    pe.wait_ge(step_ready, n)
                    for m in range(2):
                        for c in range(2):
                            mm = pe.matmul(psX[:, m * P:(m + 1) * P], wq[:, c, m * P:(m + 1) * P], xT1[:, c, :],
                                           start=(c == 0), stop=(c == 1))
                    mm.then_inc(step_mm, 1)

            def epi(tau, e, n):
                if e in (0, 7):
                    wait_apart(pe, step_ready, n)
                else:
                    pe.wait_ge(step_ready, n)
                if e == 0:
                    wait_apart(pe, on_ready, tau + 1)
                    transposes(lambda b: on[:, b].rearrange("p g d -> p (g d)"), BT, 64)
                elif e == 1:
                    for c in range(4):
                        mm = pe.matmul(psX[:, 0:D], oT[:, c], wo[:, c, :], start=(c == 0), stop=(c == 3))
                    mm.then_inc(step_mm, 1)
                elif e == 2:
                    transposes(lambda i: xn2[:, i * P:(i + 1) * P], 2)
                elif e in (3, 4):
                    w = 2 * D if e == 3 else D
                    o = 0 if e == 3 else 2 * D
                    for c in range(2):
                        mm = pe.matmul(psX[:, 0:w], xT2[:, c, :], wqkv[:, c, o:o + w], start=(c == 0), stop=(c == 1))
                    mm.then_inc(step_mm, 1)
                elif e == 5:
                    transposes(lambda i: rot[:, i * P:(i + 1) * P], 4)
                elif e == 6:
                    pe.wait_ge(q2_ready, tau + 1)
                    pe.matmul(psX[:, :], ident_r[:], causal_r[:].unsqueeze(1).to_broadcast([P, H, Q]),
                              start=True, stop=False, skip_group_check=True)
                    for b in range(BT):
                        for c in range(2):
                            mm = pe.matmul(psX[b * Q:(b + 1) * Q, c * 256:(c + 1) * 256],
                                           qkT[:, 2 + c, b * Q:(b + 1) * Q], qblk2[:, c, b], start=False, stop=True,
                                           skip_group_check=True)
                    mm.then_inc(step_mm, 1)
                elif e == 7:
                    for h in range(H):
                        for b in range(BT):
                            s = slice(b * Q, (b + 1) * Q)
                            mm = pe.matmul(psX[s, h * (DH + 1):(h + 1) * (DH + 1)], pT2[s, h * Q:(h + 1) * Q],
                                           v2[s, h, :], start=(h == 0), stop=True,
                                           skip_group_check=True)
                    mm.then_inc(step_mm, 1)
                elif e == 8:
                    transposes(lambda i: o2[:, i * P:(i + 1) * P], 2)
                elif e == 9:
                    for c in range(2):
                        mm = pe.matmul(psX[:, 0:D], o2T[:, c, :], wout[:, c, :], start=(c == 0), stop=(c == 1))
                    mm.then_inc(step_mm, 1)

            def slot(tau, b, where, first, last):
                at = step_at(tau, b, where, first, last)
                if not at:
                    return
                s, n = at
                if isinstance(s, str):
                    p_step(tau + 1, int(s[1]), n)
                else:
                    epi(tau - lag(s), s, n)

            def body(tau, par, first, last):
                for b in range(BT):
                    g = 4 * tau + b
                    score_rows(g, b % 2, 0, first=first and b == 0)
                    slot(tau, b, 0, first, last)
                    if not (last and b == 3):
                        if b < 3:
                            keys(tau, par, b + 1)
                        else:
                            keys(tau + 1, 1 - par, 0)
                    score_rows(g, b % 2, 1)
                    if b < 3:
                        slot(tau, b, 1, first, last)
                    if b > 0:
                        weigh(g - 1, (b - 1) % 2, b - 1, tau, first)
                    elif not first:
                        weigh(g - 1, 1, 3, tau - 1, False)
                    if b == 3:
                        slot(tau, b, 1, first, last)
                    if b < 3:
                        values(tau, par, b + 1)
                    elif not last:
                        values(tau + 1, 1 - par, 0)
                    slot(tau, b, 2, first, last)
                    score_cols(g, b % 2, par, b, first=first and b == 0)
                    slot(tau, b, 3, first, last)

            p_step(0, 0, None)
            p_step(0, 1, 1)
            keys(0, 0, 0, first=True)
            values(0, 0, 0)
            over_tiles(pe, body)
            weigh(4 * LAST + 3, 1, 3, LAST, False)
            for e, tau, n in final_steps():
                epi(tau, e, n)




def experts(nc, X, st3, ident, mhalf, xs, ys, WrT, W1T, W2T, tri_d, rev_d, count_d, id_d, out):
    TILES = X.shape[1]
    NS = SLOT_TILES(TILES)
    FC = F // P
    GS = min(8, TILES // 2)
    N_XS = -(-TILES // GS)

    with ExitStack() as ctx:
        def sb(name, shape, dt=F32):
            return ctx.enter_context(nc.sbuf_tensor(name, shape, dt))

        def pb(name, shape, dt=F32):
            return ctx.enter_context(nc.psum_tensor(name, shape, dt))

        def sem(name):
            return ctx.enter_context(nc.semaphore(name))

        XN = sb("XN", [P, TILES, D])
        w1 = sb("w1", [P, E, 2, 2 * F])
        w2 = sb("w2", [P, E, FC, D])
        wr = sb("wr", [P, 2, E])
        tri = sb("tri", [P, P])
        ones = sb("ones", [P, P])
        rev = sb("rev", [P, E])
        count = sb("count", [P, P])
        tid = sb("tid", [P, TILES])
        mean3 = sb("mean3", [P, TILES])
        sq3 = sb("sq3", [P, TILES])
        half3 = sb("half3", [P, TILES])
        var3 = sb("var3", [P, TILES])
        ve3 = sb("ve3", [P, TILES])
        rstd3 = sb("rstd3", [P, TILES])
        xbT = sb("xbT", [P, 2, 2, P])
        lg = sb("lg", [P, TILES, E])
        lm = sb("lm", [P, TILES, E])
        eq = sb("eq", [P, TILES, E])
        top = sb("top", [P, K, TILES])
        first = sb("first", [P, K, TILES])
        hot = sb("hot", [P, K, TILES, E])
        both = sb("both", [P, TILES, E])
        gap = sb("gap", [P, TILES])
        egap = sb("egap", [P, TILES])
        wgt = sb("wgt", [P, K, TILES])
        scan = sb("scan", [P, 2, TILES, E])
        cnt_i = sb("cnt_i", [P, E], I32)
        cnt_t = sb("cnt_t", [P, E], I32)
        nt = sb("nt", [P, E])
        escan = sb("escan", [P, 2, E])
        base = sb("base", [P, E])
        posf = sb("posf", [P, K, TILES])
        pos = sb("pos", [P, K, TILES], U32)
        posi = sb("posi", [P, K, TILES], I32)
        seat_i = sb("seat_i", [P, K, TILES], I32)
        stile_i = sb("stile_i", [P, K, TILES], I32)
        seat = sb("seat", [P, K, TILES])
        stile = sb("stile", [P, K, TILES])
        tok = sb("tok", [P, NS], U32)
        yrow = sb("yrow", [P, 2, D])
        past = sb("past", [1, NS, E])
        tef = sb("tef", [1, NS])
        te = sb("te", [1, NS], I32)
        xrow = sb("xrow", [P, 2, D])
        w1t = sb("w1t", [P, 2, 2, 2 * F])
        sg = sb("sg", [P, 2, FC, P])
        am = sb("am", [P, 2, FC, P])

        posE, tot, xsT = lm, both, xbT

        seats = XN[:].rearrange("p i d -> p (i d)").rearrange("p (k i n) -> p k i n", k=K, n=P)
        named = w1t[:].rearrange("p a c n -> p (a c n)")[:, 0:TILES * NS].rearrange("p (i t) -> p i t", i=TILES)
        picked = XN[:].rearrange("p i d -> p (i d)")[:, 0:GS * K * D].rearrange("p (s k d) -> p s k d", s=GS, k=K)

        psT = pb("psT", [P, 512])
        psT2 = pb("psT2", [P, 512])
        psL = pb("psL", [P, 512])
        psG = [pb(f"psG{i}", [P, 512]) for i in range(2)]
        psV = [pb(f"psV{i}", [P, 512]) for i in range(2)]
        psY = pb("psY", [P, 512])

        def tokens(bank):
            return bank[:, :].rearrange("p (c n) -> p c n", c=FC)

        r_in = sem("r_in")
        w_in = sem("w_in2")
        ones_set = sem("ones_set2")
        var3_ready = sem("var3_ready")
        rstd_ready = sem("rstd_ready")
        xb_ready = sem("xb_ready")
        xb_mm = sem("xb_mm")
        xbT_ready = sem("xbT_ready")
        lg_mm = sem("lg_mm")
        gap_ready = sem("gap_ready")
        exp_ready = sem("exp_ready")
        both_ready = sem("both_ready")
        rank_mm = sem("rank_mm")
        pos_ready = sem("pos_ready")
        te_ready = sem("te_ready")
        xs_out = sem("xs_out")
        seats_ready = sem("seats_ready")
        named_ready = sem("named_ready")
        named_used = sem("named_used")
        tok_ready = sem("tok_ready")
        dve_chain = sem("dve_chain2")
        pool_chain = sem("pool_chain2")
        xrow_in = [sem("xrow_in0"), sem("xrow_in1")]
        w1t_ready = [sem("w1t_ready0"), sem("w1t_ready1")]
        tx_mm = sem("tx_mm")
        xT_ready = sem("xT_ready")
        h_mm = sem("h_mm")
        silu_done = sem("silu_done")
        act_ready = sem("act_ready")
        y_mm = sem("y_mm")
        y_ready = sem("y_ready")
        y_out = [sem("y_out0"), sem("y_out1")]
        picked_in = [sem(f"picked_in{s}") for s in range(GS)]
        summed = sem("summed")
        row_out = [sem(f"row_out{s}") for s in range(GS)]

        block = ctx.enter_context(nc.Block())

        @block.sync
        def _(sp):
            for dst, src in ((wr, WrT), (tri, tri_d), (rev, rev_d), (count, count_d), (tid, id_d)):
                sp.dma_start(dst[:], src).then_inc(r_in, 16)
            for e in range(E):
                sp.dma_start(w1[:, e], W1T[:, e]).then_inc(w_in, 16)
                sp.dma_start(w2[:, e], W2T[:, e]).then_inc(w_in, 16)
            rows_of = xs.rearrange("(i p) d -> p i d", p=P)
            for i in range(0, TILES, GS):
                sp.wait_ge(xb_ready, min(i + GS, TILES))
                sp.dma_start(rows_of[:, i:min(i + GS, TILES), :], XN[:, i:min(i + GS, TILES), :]).then_inc(xs_out, 16)

            def store(t, par):
                sp.wait_ge(y_ready, t + 1)
                sp.dma_start(ys[bass.ds(t * P, P), :], yrow[:, par]).then_inc(y_out[par], 16)

            with sp.Fori(0, NS // 2) as j:
                store(2 * j, 0)
                store(2 * j + 1, 1)
            with sp.Fori(0, TILES // GS) as j:
                for s in range(GS):
                    sp.wait_ge(summed, GS * j + s + 1)
                    sp.dma_start(out[bass.ds((GS * j + s) * P, P), :], picked[:, s, 0, :]).then_inc(row_out[s], 16)
            for s in range(GS):
                sp.wait_ge(row_out[s], 16 * (TILES // GS))

        @block.gpsimd
        def _(pool):
            chain = Chain(pool, pool_chain)
            pool.wait_ge(var3_ready, 1)
            chain.done(pool.tensor_scalar(ve3[:], var3[:], EPS, None, ALU.add))
            pool.tensor_tensor(rstd3[:], ve3[:], mhalf[:].to_broadcast([P, TILES]), ALU.pow).then_inc(rstd_ready, 1)
            pool.wait_ge(xs_out, 16 * N_XS)
            pool.wait_ge(tok_ready, 1)
            for t in range(NS):
                if t >= 2:
                    pool.wait_ge(tx_mm, t - 1)
                pool.indirect_dma_start(xrow[:, t % 2, :], None, xs,
                                        bass.IndirectOffsetOnAxis(ap=tok[:, t:t + 1], axis=0)
                                        ).then_inc(xrow_in[t % 2], 16)
            pool.wait_ge(pos_ready, 1)
            for par in range(2):
                pool.wait_ge(y_out[par], 16 * (NS // 2))
            for i in range(TILES):
                s = i % GS
                if i >= GS:
                    pool.wait_ge(row_out[s], 16 * (i // GS))
                for k in range(K):
                    pool.indirect_dma_start(picked[:, s, k, :], None, ys,
                                            bass.IndirectOffsetOnAxis(ap=pos[:, k, i:i + 1], axis=0)
                                            ).then_inc(picked_in[s], 16)

        @block.scalar
        def _(act):
            with act.Fori(0, TILES // 2) as j:
                for par in range(2):
                    act.wait_ge(xb_mm, 2 * j + par + 1)
                    act.activation(xbT[:, par], (psT, psT2)[par][:, 0:D].rearrange("p (c n) -> p c n", c=2),
                                   ACT.Identity).then_inc(xbT_ready, 1)
            act.wait_ge(gap_ready, 1)
            act.activation(egap[:], gap[:], ACT.Exp).then_inc(exp_ready, 1)

            def rows(t, par, head):
                act.wait_ge(tx_mm, t + 1)
                if not head:
                    act.wait_ge(h_mm, 2 * (t - 1))
                act.activation(xsT[:, par], psT[:, 0:D].rearrange("p (c n) -> p c n", c=2),
                               ACT.Identity).then_inc(xT_ready, 1)

            def silu(t, par, head):
                act.wait_ge(h_mm, 2 * t + 1)
                if not head:
                    act.wait_ge(act_ready, t - 1)
                act.activation(sg[:, par], tokens(psG[par]), ACT.Silu).then_inc(silu_done, 1)

            def weights(t, par, head):
                if not head:
                    act.wait_ge(h_mm, 2 * (t - 1))
                e = act.value_load(te[0:1, bass.ds(t, 1)], min_val=0, max_val=E - 1)
                act.activation(w1t[:, par, 1, :], w1[:, bass.ds(e, 1), 1, :].rearrange("p a n -> p (a n)"),
                               ACT.Identity).then_inc(w1t_ready[1], 1)

            act.wait_ge(te_ready, 1)
            act.wait_ge(tok_ready, 1)
            act.wait_ge(w_in, 16 * 2 * E)
            weights(0, 0, True)
            weights(1, 1, True)
            rows(0, 0, True)
            rows(1, 1, True)
            silu(0, 0, True)
            weights(2, 0, False)
            rows(2, 0, False)
            silu(1, 1, True)
            weights(3, 1, False)
            rows(3, 1, False)
            silu(2, 0, False)
            weights(4, 0, False)
            with act.Fori(0, (NS - 6) // 2) as j:
                for par in (1, 0):
                    t = 2 * j + 4 - par
                    rows(t + 1, 1 - par, False)
                    silu(t, par, False)
                    weights(t + 2, par, False)
            rows(NS - 2, 0, False)
            silu(NS - 3, 1, False)
            weights(NS - 1, 1, False)
            rows(NS - 1, 1, False)
            silu(NS - 2, 0, False)
            silu(NS - 1, 1, False)

        @block.vector
        def _(dve):
            chain = Chain(dve, dve_chain)
            dve.memset(ones[:], 1.0).then_inc(ones_set, 1)
            dve.tensor_tensor(mean3[:], st3[:, :, 1], st3[:, :, 4], ALU.add)
            dve.tensor_tensor(sq3[:], st3[:, :, 2], st3[:, :, 5], ALU.add)
            chain.done(dve.tensor_tensor(half3[:], st3[:, :, 1], st3[:, :, 4], ALU.subtract))
            dve.tensor_tensor(half3[:], half3[:], half3[:], ALU.mult)
            chain.done(dve.tensor_scalar(mean3[:], mean3[:], 0.5, None, ALU.mult))
            chain.done(dve.tensor_scalar(half3[:], half3[:], 0.25, None, ALU.mult))
            dve.scalar_tensor_tensor(var3[:], sq3[:], 1.0 / D, half3[:], ALU.mult, ALU.add).then_inc(var3_ready, 1)
            dve.wait_ge(rstd_ready, 1)

            with dve.Fori(0, TILES) as i:
                def tile(buf):
                    return buf[:, bass.ds(i, 1), :].rearrange("p a d -> p (a d)")
                dve.tensor_scalar(tile(XN), tile(X), mean3[:, bass.ds(i, 1)], rstd3[:, bass.ds(i, 1)], ALU.subtract,
                                  ALU.mult).then_inc(xb_ready, 1)
            dve.wait_ge(r_in, 16 * 5)

            dve.wait_ge(lg_mm, TILES)
            chain.done(dve.tensor_copy(lg[:], psL[:, 0:TILES * E].rearrange("p (i e) -> p i e", e=E)))
            rv = rev[:].unsqueeze(1).to_broadcast([P, TILES, E])
            cur = lg
            for k in range(K):
                chain.done(dve.reduce_max(top[:, k], cur[:], AX_X))
                chain.done(dve.tensor_tensor(eq[:], cur[:], top[:, k].unsqueeze(2).to_broadcast([P, TILES, E]),
                                             ALU.is_equal))
                chain.done(dve.tensor_tensor(eq[:], eq[:], rv, ALU.mult))
                chain.done(dve.reduce_max(first[:, k], eq[:], AX_X))
                chain.done(dve.tensor_tensor(hot[:, k], rv, first[:, k].unsqueeze(2).to_broadcast([P, TILES, E]),
                                             ALU.is_equal))
                if k == 0:
                    chain.done(dve.scalar_tensor_tensor(lm[:], hot[:, 0], -3e38, lg[:], ALU.mult, ALU.add))
                    cur = lm
            dve.tensor_tensor(gap[:], top[:, 1], top[:, 0], ALU.subtract).then_inc(gap_ready, 1)
            dve.tensor_tensor(both[:], hot[:, 0], hot[:, 1], ALU.add).then_inc(both_ready, 1)
            dve.wait_ge(exp_ready, 1)
            chain.done(dve.tensor_scalar(gap[:], egap[:], 1.0, None, ALU.add))
            chain.done(dve.reciprocal(wgt[:, 0], gap[:]))
            chain.done(dve.tensor_tensor(wgt[:, 1], egap[:], wgt[:, 0], ALU.mult))

            dve.wait_ge(rank_mm, 1)
            chain.done(dve.tensor_copy(tot[:], psG[0][:, TILES * E:2 * TILES * E].rearrange("p (i e) -> p i e", e=E)))
            chain.done(dve.tensor_copy(scan[:, 0], tot[:]))
            a, s = 0, 1
            while s < TILES:
                dve.tensor_copy(scan[:, 1 - a, 0:s], scan[:, a, 0:s])
                chain.done(dve.tensor_tensor(scan[:, 1 - a, s:TILES], scan[:, a, s:TILES],
                                             scan[:, a, 0:TILES - s], ALU.add))
                a, s = 1 - a, 2 * s
            chain.done(dve.tensor_scalar(cnt_i[:], scan[:, a, TILES - 1], float(P - 1), None, ALU.add))
            chain.done(dve.tensor_scalar(cnt_t[:], cnt_i[:], 7, None, ALU.logical_shift_right))
            chain.done(dve.tensor_copy(nt[:], cnt_t[:]))
            chain.done(dve.tensor_copy(escan[:, 0], nt[:]))
            b, s = 0, 1
            while s < E:
                dve.tensor_copy(escan[:, 1 - b, 0:s], escan[:, b, 0:s])
                chain.done(dve.tensor_tensor(escan[:, 1 - b, s:E], escan[:, b, s:E], escan[:, b, 0:E - s], ALU.add))
                b, s = 1 - b, 2 * s
            chain.done(dve.tensor_tensor(base[:], escan[:, b], nt[:], ALU.subtract))
            chain.done(dve.tensor_scalar(base[:], base[:], float(P), None, ALU.mult))
            chain.done(dve.tensor_tensor(posE[:], scan[:, a], tot[:], ALU.subtract))
            chain.done(dve.tensor_tensor(posE[:], posE[:],
                                         psG[0][:, 0:TILES * E].rearrange("p (i e) -> p i e", e=E), ALU.add))
            chain.done(dve.tensor_tensor(posE[:], posE[:], base[:].unsqueeze(1).to_broadcast([P, TILES, E]), ALU.add))
            for k in range(K):
                chain.done(dve.tensor_tensor(eq[:], hot[:, k], posE[:], ALU.mult))
                chain.done(dve.reduce_sum(posf[:, k], eq[:], AX_X))
            dve.tensor_copy(pos[:], posf[:]).then_inc(pos_ready, 1)
            chain.done(dve.tensor_copy(posi[:], posf[:]))
            chain.done(dve.tensor_scalar(stile_i[:], posi[:], 7, None, ALU.logical_shift_right))
            chain.done(dve.tensor_scalar(seat_i[:], stile_i[:], 7, None, ALU.logical_shift_left))
            chain.done(dve.tensor_copy(stile[:], stile_i[:]))
            chain.done(dve.tensor_copy(seat[:], seat_i[:]))
            chain.done(dve.tensor_tensor(seat[:], posf[:], seat[:], ALU.subtract))
            chain.done(dve.tensor_tensor(past[:], count[0:1, 0:NS].unsqueeze(2).to_broadcast([1, NS, E]),
                                         escan[0:1, b].unsqueeze(1).to_broadcast([1, NS, E]), ALU.is_ge))
            chain.done(dve.reduce_sum(tef[:], past[:], AX_X))
            dve.tensor_scalar(te[:], tef[:], float(E - 1), None, ALU.min).then_inc(te_ready, 1)

            dve.wait_ge(xs_out, 16 * N_XS)
            for k in range(K):
                with dve.Fori(0, TILES // GS) as j:
                    dve.tensor_tensor(seats[:, k, bass.ds(GS * j, GS), :],
                                      seat[:, k, bass.ds(GS * j, GS)].unsqueeze(2).to_broadcast([P, GS, P]),
                                      count[:].unsqueeze(1).to_broadcast([P, GS, P]),
                                      ALU.is_equal).then_inc(seats_ready, 1)
                    for s in range(GS):
                        i = GS * j + s
                        if k > 0:
                            dve.wait_ge(named_used, i + 1)
                        dve.tensor_scalar(named[:, bass.ds(i, 1), :].rearrange("p a t -> p (a t)"), count[:, 0:NS],
                                          stile[:, k, bass.ds(i, 1)], tid[:, bass.ds(i, 1)], ALU.is_equal,
                                          ALU.mult).then_inc(named_ready, 1)
            dve.wait_ge(named_used, K * TILES)
            dve.tensor_copy(tok[:], psL[:, 0:NS]).then_inc(tok_ready, 1)

            def gate(t, par, head):
                dve.wait_ge(silu_done, t + 1)
                dve.wait_ge(h_mm, 2 * t + 2)
                if not head:
                    dve.wait_ge(y_mm, t - 1)
                dve.tensor_tensor(am[:, par], tokens(psV[par]), sg[:, par], ALU.mult).then_inc(act_ready, 1)

            def result(t, par, j1, head):
                dve.wait_ge(y_mm, t + 1)
                if not head:
                    dve.wait_ge(y_out[par], j1)
                dve.tensor_copy(yrow[:, par], psY[:, 0:D]).then_inc(y_ready, 1)

            def weights(t, par, head):
                if not head:
                    dve.wait_ge(h_mm, 2 * (t - 1))
                e = dve.value_load(te[0:1, bass.ds(t, 1)], min_val=0, max_val=E - 1)
                dve.tensor_copy(w1t[:, par, 0, :],
                                w1[:, bass.ds(e, 1), 0, :].rearrange("p a n -> p (a n)")).then_inc(w1t_ready[0], 1)

            dve.wait_ge(te_ready, 1)
            dve.wait_ge(w_in, 16 * 2 * E)
            weights(0, 0, True)
            weights(1, 1, True)
            gate(0, 0, True)
            weights(2, 0, False)
            gate(1, 1, True)
            weights(3, 1, False)
            result(0, 0, 0, True)
            gate(2, 0, False)
            weights(4, 0, False)
            result(1, 1, 0, True)
            with dve.Fori(0, (NS - 6) // 2) as j:
                gate(2 * j + 3, 1, False)
                weights(2 * j + 5, 1, False)
                result(2 * j + 2, 0, 16 * (j + 1), False)
                gate(2 * j + 4, 0, False)
                weights(2 * j + 6, 0, False)
                result(2 * j + 3, 1, 16 * (j + 1), False)
            gate(NS - 3, 1, False)
            weights(NS - 1, 1, False)
            result(NS - 4, 0, 16 * (NS // 2 - 2), False)
            gate(NS - 2, 0, False)
            result(NS - 3, 1, 16 * (NS // 2 - 2), False)
            gate(NS - 1, 1, False)
            result(NS - 2, 0, 16 * (NS // 2 - 1), False)
            result(NS - 1, 1, 16 * (NS // 2 - 1), False)
            links = chain.n + chain.base
            with dve.Fori(0, TILES // GS) as j:
                chain.n, chain.base = 0, links + GS * j
                for s in range(GS):
                    i = GS * j + s
                    dve.wait_ge(picked_in[s], 16 * K * (j + 1))
                    acc = picked[:, s, 0, :]
                    xi = X[:, bass.ds(i, 1), :].rearrange("p a d -> p (a d)")
                    chain.done(dve.scalar_tensor_tensor(acc, acc, wgt[:, 0, bass.ds(i, 1)], xi, ALU.mult, ALU.add))
                    dve.scalar_tensor_tensor(acc, picked[:, s, 1, :], wgt[:, 1, bass.ds(i, 1)], acc, ALU.mult,
                                             ALU.add).then_inc(summed, 1)

        @block.tensor
        def _(pe):
            pe.wait_ge(r_in, 16 * 5)
            pe.wait_ge(ones_set, 1)

            def rowsT(i):
                pe.wait_ge(xb_ready, i + 1)
                if i >= 2:
                    pe.wait_ge(xbT_ready, i - 1)
                for c in range(2):
                    mm = pe.transpose((psT, psT2)[i % 2][:, c * P:(c + 1) * P], XN[:, i, c * P:(c + 1) * P], ident[:])
                mm.then_inc(xb_mm, 1)

            def logits(i):
                pe.wait_ge(xbT_ready, i + 1)
                for c in range(2):
                    mm = pe.matmul(psL[:, i * E:(i + 1) * E], xbT[:, i % 2, c, :], wr[:, c, :], start=(c == 0),
                                   stop=(c == 1))
                mm.then_inc(lg_mm, 1)

            rowsT(0)
            for i in range(TILES):
                if i + 1 < TILES:
                    rowsT(i + 1)
                logits(i)
            pe.wait_ge(both_ready, 1)
            bv = both[:].rearrange("p i e -> p (i e)")
            pe.matmul(psG[0][:, 0:TILES * E], tri[:], bv, start=True, stop=True)
            pe.matmul(psG[0][:, TILES * E:2 * TILES * E], ones[:], bv, start=True, stop=True).then_inc(rank_mm, 1)
            for k in range(K):
                for i in range(TILES):
                    pe.wait_ge(seats_ready, (k * TILES + i) // GS + 1)
                    pe.wait_ge(named_ready, k * TILES + i + 1)
                    pe.matmul(psL[:, 0:NS], seats[:, k, i, :], named[:, i, :], start=(k == 0 and i == 0),
                              stop=(k == K - 1 and i == TILES - 1)).then_inc(named_used, 1)
            pe.wait_ge(te_ready, 1)
            pe.wait_ge(w_in, 16 * 2 * E)

            def rows(t, par, j1, head):
                pe.wait_ge(xrow_in[par], j1)
                if not head:
                    pe.wait_ge(xT_ready, t)
                for c in range(2):
                    mm = pe.transpose(psT[:, c * P:(c + 1) * P], xrow[:, par, c * P:(c + 1) * P], ident[:])
                mm.then_inc(tx_mm, 1)

            def up(t, par, head):
                pe.wait_ge(w1t_ready[0], t + 1)
                pe.wait_ge(w1t_ready[1], t + 1)
                pe.wait_ge(xT_ready, t + 1)
                if not head:
                    pe.wait_ge(act_ready, t - 1)
                for bank, o in ((psG[par], F), (psV[par], 0)):
                    for m in range(FC):
                        for c in range(2):
                            mm = pe.matmul(bank[:, m * P:(m + 1) * P],
                                           w1t[:, par, c, o + m * P:o + (m + 1) * P], xsT[:, par, c, :],
                                           start=(c == 0), stop=(c == 1))
                    mm.then_inc(h_mm, 1)

            def down(t, par, e, head):
                pe.wait_ge(act_ready, t + 1)
                if not head:
                    pe.wait_ge(y_ready, t)
                for c in range(FC):
                    mm = pe.matmul(psY[:, 0:D], am[:, par, c, :], w2[:, bass.ds(e, 1), c, :],
                                   start=(c == 0), stop=(c == FC - 1))
                mm.then_inc(y_mm, 1)

            def expert(t):
                return pe.value_load(te[0:1, bass.ds(t, 1)], min_val=0, max_val=E - 1)

            rows(0, 0, 16, True)
            rows(1, 1, 16, False)
            up(0, 0, True)
            rows(2, 0, 32, False)
            up(1, 1, True)
            down(0, 0, expert(0), True)
            rows(3, 1, 32, False)
            up(2, 0, False)
            down(1, 1, expert(1), False)
            with pe.Fori(0, (NS - 4) // 2) as j:
                for par in range(2):
                    t = 2 * j + 3 + par
                    rows(t + 1, par, 16 * (j + 3), False)
                    up(t, 1 - par, False)
                    down(t - 1, par, expert(t - 1), False)
            up(NS - 1, 1, False)
            down(NS - 2, 0, expert(NS - 2), False)
            down(NS - 1, 1, expert(NS - 1), False)



def kernel(x, ctx_512, L0_xattn_Wq, L0_xattn_bq, L0_xattn_Wk, L0_xattn_bk, L0_xattn_Wv, L0_xattn_bv, L0_xattn_Wo,
           L0_xattn_bo, L0_attn_W_qkv, L0_attn_W_out, L0_attn_b_out, L0_ffn_Wr, L0_ffn_W1, L0_ffn_W2):
    import numpy as np
    import concourse.bacc as bacc
    from concourse.bass_utils import run_bass_kernel_spmd

    x = np.asarray(x)
    B = x.shape[0]
    tiles = B * Q // P

    def rows(w):
        return np.asarray(w).reshape(-1, P, w.shape[-1]).transpose(1, 0, 2)

    def spread(b):
        return np.broadcast_to(np.asarray(b), (P, D))

    pos = np.arange(P) % Q
    ang = pos[:, None].astype(np.float32) * (1.0 / 10000.0 ** (np.arange(DH // 2, dtype=np.float32) / (DH // 2)))
    ang = ang.astype(np.float32)
    cos, sin = np.cos(ang), np.sin(ang)
    arrays = {
        "x": x.reshape(tiles, P, D).transpose(1, 0, 2),
        "ctxT": np.asarray(ctx_512).transpose(2, 0, 1).reshape(CD, -1),
        "Wq": rows(L0_xattn_Wq),
        "bq": np.asarray(L0_xattn_bq).reshape(2, P).T,
        "Wk": np.asarray(L0_xattn_Wk),
        "bk": np.asarray(L0_xattn_bk).reshape(2, P).T,
        "Wv": np.asarray(L0_xattn_Wv),
        "bvT": np.asarray(L0_xattn_bv).reshape(4, 4, DH).transpose(0, 2, 1).reshape(4 * DH, 4),
        "WoR": np.asarray(L0_xattn_Wo).reshape(4, 4, DH, D).transpose(0, 2, 1, 3).reshape(4 * DH, 4, D),
        "bo": spread(L0_xattn_bo),
        "Wqkv": rows(L0_attn_W_qkv),
        "Wout": rows(L0_attn_W_out),
        "bout": spread(L0_attn_b_out),
        "ident": np.eye(P, dtype=np.float32),
        "hmask": (np.arange(P)[:, None] // DH == np.arange(HC)[None]).astype(np.float32),
        "cos": np.stack([cos, cos], -1).reshape(P, DH),
        "sin": np.stack([-sin, sin], -1).reshape(P, DH),
        "causal": np.where(np.arange(Q)[None] >= pos[:, None], 0, -1e9 * DH ** 0.5).astype(np.float32),
        "fold": -(np.arange(P)[:, None] % Q == np.arange(Q)[None]).astype(np.float32),
        "hsel": (np.arange(P)[:, None] % Q == np.arange(H)[None]).astype(np.float32),
        "chead": (np.arange(P)[:, None] // Q == np.arange(BT)[None]).astype(np.float32),
        "WrT": np.asarray(L0_ffn_Wr).T.reshape(2, P, E).transpose(1, 0, 2),
        "W1T": np.asarray(L0_ffn_W1).transpose(2, 0, 1).reshape(2, P, E, 2 * F).transpose(1, 2, 0, 3),
        "W2T": np.asarray(L0_ffn_W2).transpose(2, 0, 1).reshape(F // P, P, E, D).transpose(1, 2, 0, 3),
        "tri": np.triu(np.ones((P, P), np.float32), 1),
        "rev": np.broadcast_to(E - np.arange(E, dtype=np.float32), (P, E)),
        "count": np.broadcast_to(np.arange(P, dtype=np.float32), (P, P)),
        "id": (np.arange(P)[:, None] + P * np.arange(tiles)[None]).astype(np.float32),
    }
    arrays = {f"in_{k}": np.ascontiguousarray(v) for k, v in arrays.items()}
    nc = bacc.Bacc("TRN2", target_bir_lowering=False, num_devices=1)
    args = [nc.dram_tensor(k, v.shape, mybir.dt.from_np(v.dtype), kind="ExternalInput").ap()
            for k, v in arrays.items()]
    out = nc.dram_tensor("out", (tiles * P, D), F32, kind="ExternalOutput").ap()
    perceiver(nc, *args, out)
    r = run_bass_kernel_spmd(nc, [arrays], core_ids=[0])
    return r.results[0]["out"].reshape(B, Q, D)
```
